# Optimizing a Trainium2 kernel written in Bass

```python
import numpy as np
import jax
import jax.numpy as jnp

def _softmax(x, axis=-1):
    return jax.nn.softmax(x, axis=axis)

def _gelu(x):
    return jax.nn.gelu(x, approximate=True)

def _silu(x):
    return jax.nn.silu(x)

def _sigmoid(x):
    return jax.nn.sigmoid(x)

def _layernorm(x, axis=-1, eps=1e-05):
    m = jnp.mean(x, axis=axis, keepdims=True)
    v = jnp.var(x, axis=axis, keepdims=True)
    return (x - m) / jnp.sqrt(v + eps)

def _scatter_add(tgt, idx, src, axis=0):
    return tgt.at[idx].add(src)

def _segment_sum(src, seg, n):
    return jax.ops.segment_sum(src, seg, n)
kernel_name = 'mk_gnn_resnorm_d2_gnn_r32_5ad580'

def setup_inputs(seed: int=0):
    np.random.seed(seed)
    _w = jnp.asarray

    def _rec_inputs():
        import jax
        import jax.numpy as jnp
        _gk = jax.random.key(seed)
        x = -0.0005121 + 1.001 * jax.random.normal(jax.random.fold_in(_gk, 1), (3125, 64), jnp.float32)
        src = jax.random.randint(jax.random.fold_in(_gk, 2), (100000,), 0, 3125, jnp.int32)
        dst = jnp.minimum((3125 * jax.random.uniform(jax.random.fold_in(_gk, 3), (100000,)) ** 2.0).astype(jnp.int32), 99999)
        _o = jnp.argsort(dst, stable=True)
        src = src[_o]
        dst = dst[_o]
        edge_attr_16 = 0.000254156 + 0.999948 * jax.random.normal(jax.random.fold_in(_gk, 11), (100000, 16), jnp.float32)
        edge_type_4 = jax.random.randint(jax.random.fold_in(_gk, 13), (100000,), 0, 4, jnp.int32)
        return (x, src, dst, edge_attr_16, edge_type_4)
    x, src, dst, edge_attr_16, edge_type_4 = _rec_inputs()

    def _L0_gnn_setup():
        import jax, jax.numpy as jnp
        import numpy as np
        N_NODES = 50000
        N_EDGES = 25000
        HID = 64
        EDGE_DIM = 16
        MSG_STEPS = 3

        def _mlp(x, W1, b1, W2, b2):
            h = jax.nn.silu(x @ W1 + b1)
            return h @ W2 + b2
        key = jax.random.key(seed)
        ks = jax.random.split(key, 12)
        s_in = lambda fan_in: 1.0 / np.sqrt(fan_in)
        node_state = jax.random.normal(ks[0], (N_NODES, HID), dtype=jnp.float32)
        edge_index = jax.random.randint(ks[1], (2, N_EDGES), 0, N_NODES, dtype=jnp.int64)
        edge_attr = jax.random.normal(ks[2], (N_EDGES, EDGE_DIM), dtype=jnp.float32)
        W1e = jax.random.normal(ks[3], (2 * HID + EDGE_DIM, HID), dtype=jnp.float32) * s_in(2 * HID + EDGE_DIM)
        b1e = jnp.zeros((HID,), dtype=jnp.float32)
        W2e = jax.random.normal(ks[4], (HID, HID), dtype=jnp.float32) * s_in(HID)
        b2e = jnp.zeros((HID,), dtype=jnp.float32)
        W1n = jax.random.normal(ks[5], (2 * HID, HID), dtype=jnp.float32) * s_in(2 * HID)
        b1n = jnp.zeros((HID,), dtype=jnp.float32)
        W2n = jax.random.normal(ks[6], (HID, HID), dtype=jnp.float32) * s_in(HID)
        b2n = jnp.zeros((HID,), dtype=jnp.float32)
        return {'node_state': node_state, 'edge_index': edge_index, 'edge_attr': edge_attr, 'W1e': W1e, 'b1e': b1e, 'W2e': W2e, 'b2e': b2e, 'W1n': W1n, 'b1n': b1n, 'W2n': W2n, 'b2n': b2n}
    _L0_gnn_all = _L0_gnn_setup()
    _L0_gnn_in = {k: v for k, v in _L0_gnn_all.items() if k in ('W1e', 'b1e', 'W2e', 'b2e', 'W1n', 'b1n', 'W2n', 'b2n')}
    del _L0_gnn_all

    def _L1_gnn_setup():
        import jax, jax.numpy as jnp
        import numpy as np
        N_NODES = 3125
        N_EDGES = 50000
        IN_CH = 64
        HID_CH = 64
        OUT_CH = 64
        NUM_REL = 4

        def _rgcn_layer(x, W, root, b, src, dst, edge_type, n_nodes):
            R = W.shape[0]
            seg = edge_type * n_nodes + dst
            msgs = x[src]
            agg = jax.ops.segment_sum(msgs, seg, num_segments=R * n_nodes)
            cnt = jax.ops.segment_sum(jnp.ones(seg.shape, x.dtype), seg, num_segments=R * n_nodes)
            agg = (agg / jnp.maximum(cnt, 1.0)[:, None]).reshape(R, n_nodes, -1)
            return x @ root + b + jnp.einsum('rni,rio->no', agg, W)
        key = jax.random.key(seed)
        ks = jax.random.split(key, 12)

        def lin(k, shape, fan_in):
            return jax.random.normal(k, shape, dtype=jnp.float32) * (1.0 / np.sqrt(fan_in))
        x = jax.random.normal(ks[0], (N_NODES, IN_CH), dtype=jnp.float32)
        edge_index = jax.random.randint(ks[1], (2, N_EDGES), 0, N_NODES, dtype=jnp.int64)
        edge_type = jax.random.randint(ks[2], (N_EDGES,), 0, NUM_REL, dtype=jnp.int64)
        return {'x': x, 'W0': lin(ks[3], (NUM_REL, IN_CH, HID_CH), IN_CH), 'root0': lin(ks[4], (IN_CH, HID_CH), IN_CH), 'b0': jnp.zeros((HID_CH,), jnp.float32), 'W1': lin(ks[5], (NUM_REL, HID_CH, HID_CH), HID_CH), 'root1': lin(ks[6], (HID_CH, HID_CH), HID_CH), 'b1': jnp.zeros((HID_CH,), jnp.float32), 'W2': lin(ks[7], (NUM_REL, HID_CH, OUT_CH), HID_CH), 'root2': lin(ks[8], (HID_CH, OUT_CH), HID_CH), 'b2': jnp.zeros((OUT_CH,), jnp.float32), 'edge_index': edge_index, 'edge_type': edge_type}
    _L1_gnn_all = _L1_gnn_setup()
    _L1_gnn_in = {k: v for k, v in _L1_gnn_all.items() if k in ('W0', 'root0', 'b0', 'W1', 'root1', 'b1', 'W2', 'root2', 'b2')}
    del _L1_gnn_all
    return {'x': x, 'src': src, 'dst': dst, 'edge_attr_16': edge_attr_16, 'edge_type_4': edge_type_4, 'L0_gnn_W1e': _L0_gnn_in['W1e'], 'L0_gnn_b1e': _L0_gnn_in['b1e'], 'L0_gnn_W2e': _L0_gnn_in['W2e'], 'L0_gnn_b2e': _L0_gnn_in['b2e'], 'L0_gnn_W1n': _L0_gnn_in['W1n'], 'L0_gnn_b1n': _L0_gnn_in['b1n'], 'L0_gnn_W2n': _L0_gnn_in['W2n'], 'L0_gnn_b2n': _L0_gnn_in['b2n'], 'L1_gnn_W0': _L1_gnn_in['W0'], 'L1_gnn_root0': _L1_gnn_in['root0'], 'L1_gnn_b0': _L1_gnn_in['b0'], 'L1_gnn_W1': _L1_gnn_in['W1'], 'L1_gnn_root1': _L1_gnn_in['root1'], 'L1_gnn_b1': _L1_gnn_in['b1'], 'L1_gnn_W2': _L1_gnn_in['W2'], 'L1_gnn_root2': _L1_gnn_in['root2'], 'L1_gnn_b2': _L1_gnn_in['b2']}

def reference(x, src, dst, edge_attr_16, edge_type_4, L0_gnn_W1e, L0_gnn_b1e, L0_gnn_W2e, L0_gnn_b2e, L0_gnn_W1n, L0_gnn_b1n, L0_gnn_W2n, L0_gnn_b2n, L1_gnn_W0, L1_gnn_root0, L1_gnn_b0, L1_gnn_W1, L1_gnn_root1, L1_gnn_b1, L1_gnn_W2, L1_gnn_root2, L1_gnn_b2):
    import jax
    import jax.numpy as jnp

    def _L0_gnn_ref(node_state, edge_index, edge_attr, W1e, b1e, W2e, b2e, W1n, b1n, W2n, b2n):
        import jax, jax.numpy as jnp
        import numpy as np
        N_NODES = 50000
        N_EDGES = 25000
        HID = 64
        EDGE_DIM = 16
        MSG_STEPS = 3

        def _mlp(x, W1, b1, W2, b2):
            h = jax.nn.silu(x @ W1 + b1)
            return h @ W2 + b2
        src, dst = (edge_index[0], edge_index[1])
        n = node_state.shape[0]
        deg = jax.ops.segment_sum(jnp.ones((dst.shape[0],), node_state.dtype), dst, num_segments=n)
        deg = jnp.maximum(deg, 1.0)[:, None]
        h = node_state
        for _ in range(MSG_STEPS):
            msg_in = jnp.concatenate([h[src], h[dst], edge_attr], axis=1)
            msg = _mlp(msg_in, W1e, b1e, W2e, b2e)
            agg = jax.ops.segment_sum(msg, dst, num_segments=n) / deg
            h = h + _mlp(jnp.concatenate([h, agg], axis=1), W1n, b1n, W2n, b2n)
        return h

    def _L1_gnn_ref(x, W0, root0, b0, W1, root1, b1, W2, root2, b2, edge_index, edge_type):
        import jax, jax.numpy as jnp
        import numpy as np
        N_NODES = 3125
        N_EDGES = 50000
        IN_CH = 64
        HID_CH = 64
        OUT_CH = 64
        NUM_REL = 4

        def _rgcn_layer(x, W, root, b, src, dst, edge_type, n_nodes):
            R = W.shape[0]
            seg = edge_type * n_nodes + dst
            msgs = x[src]
            agg = jax.ops.segment_sum(msgs, seg, num_segments=R * n_nodes)
            cnt = jax.ops.segment_sum(jnp.ones(seg.shape, x.dtype), seg, num_segments=R * n_nodes)
            agg = (agg / jnp.maximum(cnt, 1.0)[:, None]).reshape(R, n_nodes, -1)
            return x @ root + b + jnp.einsum('rni,rio->no', agg, W)
        src, dst = (edge_index[0], edge_index[1])
        n = x.shape[0]
        h = jax.nn.relu(_rgcn_layer(x, W0, root0, b0, src, dst, edge_type, n))
        h = jax.nn.relu(_rgcn_layer(h, W1, root1, b1, src, dst, edge_type, n))
        return _rgcn_layer(h, W2, root2, b2, src, dst, edge_type, n)
    edge_index = jnp.stack([src, dst])
    x = _layernorm(x + _L0_gnn_ref(x, edge_index, edge_attr_16, L0_gnn_W1e, L0_gnn_b1e, L0_gnn_W2e, L0_gnn_b2e, L0_gnn_W1n, L0_gnn_b1n, L0_gnn_W2n, L0_gnn_b2n), axis=-1)
    x = _layernorm(x + _L1_gnn_ref(x, L1_gnn_W0, L1_gnn_root0, L1_gnn_b0, L1_gnn_W1, L1_gnn_root1, L1_gnn_b1, L1_gnn_W2, L1_gnn_root2, L1_gnn_b2, edge_index, edge_type_4), axis=-1)
    return x

_drawn_inputs = setup_inputs


def setup_inputs(seed=0):
    import zlib

    import numpy as np

    out = dict(_drawn_inputs(seed))
    spreads = {'L0_gnn_b1e': (0.0, 0.1),
     'L0_gnn_b2e': (0.0, 0.1),
     'L0_gnn_b1n': (0.0, 0.1),
     'L0_gnn_b2n': (0.0, 0.1),
     'L1_gnn_b0': (0.0, 0.1),
     'L1_gnn_b1': (0.0, 0.1),
     'L1_gnn_b2': (0.0, 0.1)}
    factors = {'edge_attr_16': 3.5}
    for name, (base, spread) in spreads.items():
        noise = np.random.default_rng([zlib.crc32(name.encode()), seed]).standard_normal(out[name].shape)
        drawn = base * np.exp(spread * noise) if base else spread * noise
        out[name] = jnp.asarray(drawn.astype(out[name].dtype))
    for name, factor in factors.items():
        out[name] = (out[name] * factor).astype(out[name].dtype)
    return out
```

```python
from contextlib import ExitStack

import concourse.bass as bass
from concourse import mybir

ALU = mybir.AluOpType
ACT = mybir.ActivationFunctionType
X_AXIS = mybir.AxisListType.X
F32 = mybir.dt.float32
BF16 = mybir.dt.bfloat16
I32 = mybir.dt.int32
U32 = mybir.dt.uint32
U16 = mybir.dt.uint16

P = 128
HID = 64
EPS = 1e-5

GT = 8
REC = HID + 4
ROW0, ROW1, PLACE, TYPE = HID, HID + 1, HID + 2, HID + 3
PER_BANK = 512 // REC


def gnn_kernel(nc, x, src, dst, edge_attr, edge_type, W1e, b1e, W2e, b2e, W1n, b1n, W2n, b2n,
               rel_w, rel_root, rel_b, out):
    N = x.shape[0]
    E, ED = edge_attr.shape
    R = rel_w[0].shape[0]
    NB = -(-N // P)
    NP = NB * P
    LAST = N - (NB - 1) * P
    EP = 125
    EC = E // EP
    EG = EC // GT
    TILES = (E + NB * (P - 1)) // P
    NG = -(-TILES // GT)
    PAIRS = NG // 2
    LAST_TILES = TILES - (NG - 1) * GT
    BANKS = -(-NB // PER_BANK)
    CH = -(-NB // 4)
    LAYERS = 3
    assert EP * EC == E and EG % 2 == 0 and NG % 2 == 1 and GT * ED == P and R == 4

    recs = nc.dram_tensor("recs", [NG * GT * P, REC], F32, kind="Internal").ap()
    table0 = nc.dram_tensor("table0", [NP, HID], F32, kind="Internal").ap()
    table1 = nc.dram_tensor("table1", [NP * R, HID], F32, kind="Internal").ap()
    recs_by_group = recs.rearrange("(g p j) w -> p g (j w)", p=P, j=GT)

    def chunk(c):
        return range(4 * c, min(4 * c + 4, NB))

    with ExitStack() as ctx:
        def sb(name, shape, dt=F32):
            return ctx.enter_context(nc.sbuf_tensor(name, shape, dt))

        def ps(name, shape, dt=F32):
            return ctx.enter_context(nc.psum_tensor(name, shape, dt))

        def sem(name):
            return ctx.enter_context(nc.semaphore(name))

        ident = sb("ident", [P, P])
        ident_b = sb("ident_b", [P, P], BF16)
        ones = sb("ones", [P, P])
        before = sb("before", [P, P])
        iota_i = sb("iota_i", [P, P], I32)
        iota_b = sb("iota_b", [P, P], BF16)
        iota_r = sb("iota_r", [P, R])
        tile_i = sb("tile_i", [P, GT], I32)
        tile_f = sb("tile_f", [P, GT])
        block_step = sb("block_step", [P, NB - 1])
        zeros_b = sb("zeros_b", [P, 512], BF16)
        ones_e = sb("ones_e", [P, EC], BF16)
        no_edge = sb("no_edge", [P, GT, REC])
        eps = sb("eps", [P, 1])
        we8 = sb("we8", [P, GT, HID])
        w_ab = sb("w_ab", [HID, 2 * HID])
        b1e_all = sb("b1e_all", [P, HID])
        w2e = sb("w2e", [HID + 1, P])
        w1n = sb("w1n", [P, HID])
        w2n = sb("w2n", [HID, HID])
        b1n_c = sb("b1n_c", [HID, 1])
        b2n_c = sb("b2n_c", [HID, 1])
        w_rel = [sb(f"w_rel{l}", [HID, R + 1, HID]) for l in range(LAYERS)]
        b_rel = [sb(f"b_rel{l}", [P, HID]) for l in range(LAYERS)]
        xn = sb("xn", [P, NB, HID])
        x1 = sb("x1", [P, NB, HID])
        hn = sb("hn", [P, NB, HID])
        cat = sb("cat", [P, NP])
        dst_terms = sb("dst_terms", [P, BANKS, 512])
        terms_flat = dst_terms[:].rearrange("p a b -> p (a b)")
        deg = sb("deg", [P, 4, NB])
        stat = sb("stat", [P, 4, NB])
        arena1 = sb("arena1", [P, 10240])
        arena2 = sb("arena2", [P, 8 * EC + 1664])
        in_block = arena1[0:EP, 0:NB * EC // 2].bitcast(BF16).rearrange("p (k e) -> p k e", k=NB)
        y_rows = arena1[:, 0:NB * R * HID].rearrange("p (b w) -> p b w", b=NB)
        root = arena1[:, NB * R * HID:NB * (R + 1) * HID].rearrange("p (b w) -> p b w", b=NB)
        v = arena1[:, NB * (R + 1) * HID:NB * (R + 2) * HID].rearrange("p (b w) -> p b w", b=NB)

        def edge_row(k, dt=F32):
            return arena2[0:EP, k * EC:(k + 1) * EC].bitcast(dt)

        src_i, dst_i, type_i, part_i = (edge_row(k, I32) for k in range(4))
        block_f, rank, slot_f = (edge_row(k) for k in range(4, 7))
        slot_i = edge_row(7, I32)
        mean_t = arena2[0:HID + 1, 0:NP]
        hidden = arena2[0:HID, NP:2 * NP]
        mean_n = arena2[:, 2 * NP:2 * NP + NB * (HID + 1)].rearrange("p (b w) -> p b w", b=NB)
        meta = sb("meta", [EP, EC, 4])
        meta_i = meta[:].bitcast(I32)
        addr = sb("addr", [EP, EC], I32)
        count = sb("count", [EP, NB])
        tiles_i = sb("tiles_i", [P, NB], I32)
        tiles_f = sb("tiles_f", [P, NB])
        tiles_end = sb("tiles_end", [P, NB])
        first_slot = sb("first_slot", [P, NB])
        passed = sb("passed", [P, GT, NB - 1])
        off_f = sb("off_f", [P, GT])
        off_i = sb("off_i", [P, GT], I32)
        offsets = sb("offsets", [1, NG * GT], I32)
        ea = [sb(f"ea{s}", [EP, P]) for s in range(2)]
        ea_t = [sb(f"ea_t{s}", [P, EP]) for s in range(2)]
        rec_out = [sb(f"rec_out{s}", [EP, GT, REC]) for s in range(2)]
        addr_out = [sb(f"addr_out{s}", [EP, GT], I32) for s in range(2)]
        rec_in = [sb(f"rec_in{s}", [P, GT, REC]) for s in range(2)]
        rows = [sb(f"rows{s}", [P, GT, HID]) for s in range(2)]
        onehot_b = [sb(f"onehot_b{s}", [P, GT, P], BF16) for s in range(2)]
        onehot = [sb(f"onehot{s}", [P, GT, P]) for s in range(2)]
        onehot_t = [sb(f"onehot_t{s}", [P, GT, P]) for s in range(2)]
        z = [sb(f"z{s}", [P, GT, HID]) for s in range(2)]
        msg = [sb(f"msg{s}", [P, GT, REC]) for s in range(2)]
        is_type = [sb(f"is_type{s}", [P, GT, R]) for s in range(2)]
        share = [sb(f"share{s}", [P, GT]) for s in range(2)]

        sums = ps("sums", [P, BANKS * 512])
        sums_v = sums[:].rearrange("p (a b) -> p a b", a=BANKS)
        work = [ps(f"work{k}", [P, 512]) for k in range(4)]
        turned = [work[s][:].bitcast(BF16) for s in range(2)]
        gathered_ps = [work[2 + s] for s in range(2)]

        def bank_blocks(c):
            return range(PER_BANK * c, min(PER_BANK * c + PER_BANK, NB))

        def bank_view(t, c, a, b):
            n = len(bank_blocks(c))
            return t[:, c, 0:n * REC].rearrange("p (i w) -> p i w", w=REC)[:, :, a:b]

        pool_step = sem("pool_step")
        consts_made = sem("consts_made")
        consts_cast = sem("consts_cast")
        weights_in = sem("weights_in")
        zeroed = sem("zeroed")
        rel_in = sem("rel_in")
        x_in = sem("x_in")
        edges_in = sem("edges_in")
        recs_blank = sem("recs_blank")
        dve_step = sem("dve_step")
        turn_mm = sem("turn_mm")
        turn_out = sem("turn_out")
        term_mm = sem("term_mm")
        src_terms_out = sem("src_terms_out")
        dst_terms_out = sem("dst_terms_out")
        table_stored = sem("table_stored")
        mean_ready = sem("mean_ready")
        mean_turned = sem("mean_turned")
        mean_t_out = sem("mean_t_out")
        agg_mm = sem("agg_mm")
        agg_out = sem("agg_out")
        hidden_mm = sem("hidden_mm")
        hidden_out = sem("hidden_out")
        delta_mm = sem("delta_mm")
        state_ready = sem("state_ready")
        back_mm = sem("back_mm")
        back_out = sem("back_out")
        var_ready = sem("var_ready")
        sd_ready = sem("sd_ready")
        normed = sem("normed")
        rel_mm = sem("rel_mm")
        y_out = sem("y_out")
        root_out = sem("root_out")
        layer_out = sem("layer_out")
        stored = sem("stored")
        counted = sem("counted")
        count_mm = sem("count_mm")
        off_ready = sem("off_ready")
        offsets_in = sem("offsets_in")
        ea_in = [sem(f"ea_in{s}") for s in range(2)]
        ea_turned = sem("ea_turned")
        ea_t_out = sem("ea_t_out")
        term_e_mm = sem("term_e_mm")
        rec_made = sem("rec_made")
        scatter_go = sem("scatter_go")
        rec_stored = [sem(f"rec_stored{s}") for s in range(2)]
        rec_loaded = [sem(f"rec_loaded{s}") for s in range(2)]
        rec_used = sem("rec_used")
        gather_go = sem("gather_go")
        rows_in = [sem(f"rows_in{s}") for s in range(2)]
        onehot_made = sem("onehot_made")
        onehot_turned = sem("onehot_turned")
        onehot_out = sem("onehot_out")
        onehot_t_out = sem("onehot_t_out")
        terms_gathered = sem("terms_gathered")
        z_ready = sem("z_ready")
        msg_ready = sem("msg_ready")
        summed = sem("summed")
        share_step = sem("share_step")

        def done(n):
            return n + 3

        def reusable(n):
            return n + 1

        USES = [PAIRS + 1, PAIRS]
        ROWS_LAYER = [16 * (GT * PAIRS + LAST_TILES), 16 * GT * PAIRS]

        def groups(eng, body):
            with eng.Fori(0, PAIRS) as i:
                body(i, 0, GT)
                body(i, 1, GT)
            body(PAIRS, 0, LAST_TILES)

        block = ctx.enter_context(nc.Block())

        @block.sync
        def _(sp):
            for t, a in ((dst_i, dst), (src_i, src), (type_i, edge_type)):
                sp.dma_start(t, a.rearrange("(p e) -> p e", p=EP)).then_inc(edges_in, 16)
            sp.wait_ge(zeroed, 1)
            sp.dma_start(xn[:, 0:NB - 1, :],
                         x[0:(NB - 1) * P, :].rearrange("(b p) f -> p b f", p=P)).then_inc(x_in, 16)
            sp.dma_start(xn[0:LAST, NB - 1, :], x[(NB - 1) * P:N, :]).then_inc(x_in, 16)

            attr = edge_attr.rearrange("(p e) f -> p (e f)", p=EP)

            def load_attr(g, s):
                sp.wait_ge(ea_turned, g + 1)
                sp.dma_start(ea[s][:], attr[:, bass.ds(g * P, P)]).then_inc(ea_in[s], 16)

            def store_table0(l):
                sp.wait_ge(src_terms_out, CH * (l + 1))
                sp.dma_start(table0.rearrange("(b p) f -> p b f", p=P), hn[:]).then_inc(table_stored, 16)

            store_table0(0)
            sp.wait_ge(off_ready, 1)
            sp.dma_start(offsets[0:1, :], off_i[0:NG, :]).then_inc(offsets_in, 16)
            with sp.Fori(0, EG // 2) as i:
                for s in range(2):
                    load_attr(2 * i + s, s)
            for s in range(2):
                sp.wait_ge(rec_stored[s], 16 * GT * (EG // 2))

            for l in range(2 * LAYERS):
                if 0 < l < LAYERS:
                    store_table0(l)
                if l >= LAYERS:
                    k = l - LAYERS
                    sp.wait_ge(y_out, NB * (k + 1))
                    sp.dma_start(table1.rearrange("(b p r) f -> p b (r f)", p=P, r=R),
                                 y_rows).then_inc(table_stored, 16)

                def load_group(i, s, nt, l=l):
                    n = l * NG + 2 * i + s
                    sp.wait_ge(rec_used, reusable(n))
                    sp.dma_start(rec_in[s][:].rearrange("p j w -> p (j w)"),
                                 recs_by_group[:, bass.ds(2 * i + s, 1), :].rearrange("p a w -> p (a w)")
                                 ).then_inc(rec_loaded[s], 16)

                groups(sp, load_group)
            sp.wait_ge(normed, 2)
            sp.dma_start(out[0:(NB - 1) * P, :].rearrange("(b p) f -> p b f", p=P),
                         hn[:, 0:NB - 1, :]).then_inc(stored, 16)
            sp.dma_start(out[(NB - 1) * P:N, :], hn[0:LAST, NB - 1, :]).then_inc(stored, 16)
            sp.wait_ge(stored, 32)

        @block.gpsimd
        def _(pool):
            pool.memset(ident[:], 0.0).then_inc(pool_step, 1)
            pool.memset(ones[:], 1.0).then_inc(pool_step, 1)
            pool.iota(iota_i[:], [[1, P]], base=0, channel_multiplier=0).then_inc(consts_made, 1)
            pool.iota(tile_i[:], [[1, GT]], base=0, channel_multiplier=GT).then_inc(consts_made, 1)
            pool.wait_ge(pool_step, 2)
            pool.affine_select(out=ident[:], in_=ident[:], compare_op=ALU.not_equal, fill=1.0,
                               base=0, pattern=[[-1, P]], channel_multiplier=1).then_inc(consts_made, 1)
            pool.affine_select(out=before[:], in_=ones[:], compare_op=ALU.is_gt, fill=0.0,
                               base=0, pattern=[[1, P]], channel_multiplier=-1).then_inc(consts_made, 1)

            pool.wait_ge(recs_blank, 16)
            with pool.Fori(0, EG // 2) as i:
                for s in range(2):
                    pool.wait_ge(rec_made, 3 * (2 * i + s) + 9)
                    pool.sem_inc(scatter_go, 1)
                    for j in range(GT):
                        pool.indirect_dma_start(
                            recs, bass.IndirectOffsetOnAxis(ap=addr_out[s][:, j:j + 1].bitcast(U32), axis=0),
                            rec_out[s][:, j, :], None).then_inc(rec_stored[s], 16)

            for l in range(2 * LAYERS):
                pool.wait_ge(table_stored, 16 * (l + 1))
                table = table0 if l < LAYERS else table1
                field = ROW0 if l < LAYERS else ROW1

                def gather(i, s, nt, l=l):
                    n = l * NG + 2 * i + s
                    pool.wait_ge(rec_used, reusable(n))
                    pool.wait_ge(rec_loaded[s], 16 * (l * USES[s] + i + 1))
                    pool.sem_inc(gather_go, 1)
                    for j in range(nt):
                        pool.indirect_dma_start(
                            rows[s][:, j, :], None, table,
                            bass.IndirectOffsetOnAxis(ap=rec_in[s][:, j, field:field + 1].bitcast(U32), axis=0)
                        ).then_inc(rows_in[s], 16)

                groups(pool, gather)

        @block.scalar
        def _(act):
            act.wait_ge(zeroed, 1)
            for i in range(GT):
                act.dma_start(we8[ED * i:ED * (i + 1), i, :], W1e[2 * HID:2 * HID + ED, :]).then_inc(weights_in, 16)
            act.dma_start(w_ab[:, 0:HID], W1e[0:HID, :]).then_inc(weights_in, 16)
            act.dma_start(w_ab[:, HID:2 * HID], W1e[HID:2 * HID, :]).then_inc(weights_in, 16)
            act.dma_start(b1e_all[:], b1e.partition_broadcast(P)).then_inc(weights_in, 16)
            act.dma_start(w2e[0:HID, HID:P], W2e).then_inc(weights_in, 16)
            act.dma_start(w2e[HID:HID + 1, HID:P], b2e.rearrange("(a f) -> a f", a=1)).then_inc(weights_in, 16)
            act.dma_start(w1n[:], W1n).then_inc(weights_in, 16)
            act.dma_start(w2n[:], W2n).then_inc(weights_in, 16)
            act.dma_start(b1n_c[:], b1n.rearrange("(f a) -> f a", a=1)).then_inc(weights_in, 16)
            act.dma_start(b2n_c[:], b2n.rearrange("(f a) -> f a", a=1)).then_inc(weights_in, 16)
            act.dma_start(recs_by_group, no_edge[:].rearrange("p j w -> p (j w)").unsqueeze(1)
                          .to_broadcast([P, NG, GT * REC])).then_inc(recs_blank, 16)
            for l in range(LAYERS):
                act.dma_start(w_rel[l][:, 0:R, :], rel_w[l].rearrange("r i o -> i r o")).then_inc(rel_in, 16)
                act.dma_start(w_rel[l][:, R, :], rel_root[l]).then_inc(rel_in, 16)
                act.dma_start(b_rel[l][:], rel_b[l].partition_broadcast(P)).then_inc(rel_in, 16)

            def turn_state(t):
                for c in range(CH):
                    w = P * len(chunk(c))
                    act.wait_ge(turn_mm, CH * t + c + 1)
                    act.copy(cat[0:HID, 512 * c:512 * c + w], work[c % 2][0:HID, 0:w]).then_inc(turn_out, 1)

            def source_terms(l):
                for c in range(CH):
                    n = len(chunk(c))
                    act.wait_ge(term_mm, CH * l + c + 1)
                    act.copy(hn[:, 4 * c:4 * c + n, :],
                             work[c % 4][:, 0:P * n].rearrange("p (b w) -> p b w", b=n)[:, :, 0:HID]
                             ).then_inc(src_terms_out, 1)

            turn_state(0)
            source_terms(0)

            for q in (ea_t_out, onehot_out, onehot_t_out):
                act.sem_inc(q, 2)
            with act.Fori(0, EG // 2) as i:
                for s in range(2):
                    g = 2 * i + s
                    act.wait_ge(ea_turned, done(g))
                    act.wait_ge(term_e_mm, reusable(g))
                    act.copy(ea_t[s][:], work[s][:, 0:EP]).then_inc(ea_t_out, 1)

            for l in range(2 * LAYERS):
                if 0 < l < LAYERS:
                    source_terms(l)
                if l >= LAYERS:
                    k = l - LAYERS
                    if k == 0:
                        act.wait_ge(var_ready, 1)
                        act.activation(stat[:, 2, :], stat[:, 1, :], ACT.Sqrt, bias=eps[:, 0:1],
                                       scale=1.0 / HID).then_inc(sd_ready, 1)
                    turn_state(1 + k)
                    for b in range(NB):
                        act.wait_ge(rel_mm, NB * k + b + 1)
                        act.copy(y_rows[:, b, :], work[b % 4][:, 0:R * HID]).then_inc(y_out, 1)

                def edge_group(i, s, nt, l=l):
                    n = l * NG + 2 * i + s
                    act.wait_ge(onehot_made, done(n))
                    act.wait_ge(summed, reusable(n))
                    act.copy(onehot[s][:], onehot_b[s][:]).then_inc(onehot_out, 1)
                    act.wait_ge(onehot_turned, done(n))
                    act.wait_ge(terms_gathered, reusable(n))
                    act.copy(onehot_t[s][:].rearrange("p j n -> p (j n)"), turned[s]).then_inc(onehot_t_out, 1)
                    if l < LAYERS:
                        act.wait_ge(z_ready, done(n))
                        act.activation(msg[s][:, :, 0:HID], z[s][:], ACT.Silu).then_inc(msg_ready, 1)

                groups(act, edge_group)

                if l < LAYERS:
                    for c in range(CH):
                        w = P * len(chunk(c))
                        act.wait_ge(mean_turned, CH * l + c + 1)
                        act.copy(mean_t[:, 512 * c:512 * c + w], work[c % 2][0:HID + 1, 0:w]).then_inc(mean_t_out, 1)
                    for c in range(CH):
                        w = P * len(chunk(c))
                        act.wait_ge(agg_mm, CH * l + c + 1)
                        act.copy(cat[HID:P, 512 * c:512 * c + w], work[2 + c % 2][HID:P, 0:w]).then_inc(agg_out, 1)
                    for c in range(CH):
                        w = P * len(chunk(c))
                        act.wait_ge(hidden_mm, CH * l + c + 1)
                        act.activation(hidden[:, 512 * c:512 * c + w], work[c % 2][0:HID, 0:w], ACT.Silu,
                                       bias=b1n_c[:, 0:1]).then_inc(hidden_out, 1)
            act.wait_ge(var_ready, 2)
            act.activation(stat[:, 2, :], stat[:, 1, :], ACT.Sqrt, bias=eps[:, 0:1],
                           scale=1.0 / HID).then_inc(sd_ready, 1)

        @block.tensor
        def _(pe):
            pe.wait_ge(consts_made, 4)
            pe.wait_ge(x_in, 32)

            def turn_state(t, nodes):
                for c in range(CH):
                    if c >= 2:
                        pe.wait_ge(turn_out, CH * t + c - 1)
                    for m, b in enumerate(chunk(c)):
                        ins = pe.transpose(work[c % 2][0:HID, m * P:(m + 1) * P], nodes[:, b, :], ident[:])
                    ins.then_inc(turn_mm, 1)

            def terms(l):
                for c in range(CH):
                    if c >= 4:
                        pe.wait_ge(src_terms_out, CH * l + c - 3)
                        pe.wait_ge(dst_terms_out, CH * l + c - 3)
                    for m, b in enumerate(chunk(c)):
                        ins = pe.matmul(work[c % 4][:, m * P:(m + 1) * P], cat[0:HID, b * P:(b + 1) * P],
                                        w_ab[:], start=True, stop=True)
                    ins.then_inc(term_mm, 1)

            turn_state(0, xn)
            pe.wait_ge(turn_out, CH)
            pe.wait_ge(weights_in, 16 * (GT + 9))
            terms(0)

            pe.wait_ge(counted, 1)
            pe.wait_ge(src_terms_out, CH)
            pe.wait_ge(dst_terms_out, CH)
            pe.matmul(work[0][0:EP, 0:NB], before[0:EP, 0:EP], count[:], start=True, stop=True)
            pe.matmul(work[1][:, 0:NB], ones[0:EP, :], count[:], start=True, stop=True).then_inc(count_mm, 1)
            pe.wait_ge(dve_step, RANKED)
            for q in (ea_turned, term_e_mm, onehot_turned, terms_gathered, summed):
                pe.sem_inc(q, 2)
            with pe.Fori(0, EG // 2) as i:
                for s in range(2):
                    g = 2 * i + s
                    pe.wait_ge(ea_in[s], 16 * (i + 1))
                    pe.wait_ge(ea_t_out, reusable(g))
                    pe.transpose(work[s][:, 0:EP], ea[s][:], ident[0:EP, 0:EP]).then_inc(ea_turned, 1)
                    pe.wait_ge(ea_t_out, done(g))
                    pe.wait_ge(rec_made, 3 * g + 1)
                    pe.matmul(work[2 + s][0:EP, :], ea_t[s][:], we8[:].rearrange("p i f -> p (i f)"),
                              start=True, stop=True).then_inc(term_e_mm, 1)

            pe.wait_ge(offsets_in, 16)
            pe.wait_ge(consts_cast, 1)
            pe.wait_ge(rec_made, 3 * EG + 6)
            for l in range(2 * LAYERS):
                if 0 < l < LAYERS:
                    pe.wait_ge(state_ready, CH * l)
                    terms(l)
                if l < LAYERS:
                    pe.wait_ge(src_terms_out, CH * (l + 1))
                    pe.wait_ge(dst_terms_out, CH * (l + 1))
                if l >= LAYERS:
                    k = l - LAYERS
                    if k == 0:
                        pe.wait_ge(rel_in, 16 * 3 * LAYERS)
                        pe.wait_ge(state_ready, CH * LAYERS)
                        for c in range(-(-NB // 8)):
                            if c >= 2:
                                pe.wait_ge(back_out, c - 1)
                            for m, b in enumerate(range(8 * c, min(8 * c + 8, NB))):
                                ins = pe.transpose(work[c % 2][:, m * HID:(m + 1) * HID],
                                                   cat[0:HID, b * P:(b + 1) * P], ident[0:HID, 0:HID])
                            ins.then_inc(back_mm, 1)
                        pe.wait_ge(normed, 1)
                    else:
                        pe.wait_ge(layer_out, k)
                    turn_state(1 + k, x1 if k == 0 else hn)
                    pe.wait_ge(turn_out, CH * (2 + k))
                    for b in range(NB):
                        if b >= 4:
                            pe.wait_ge(y_out, NB * k + b - 3)
                            pe.wait_ge(root_out, NB * k + b - 3)
                        pe.matmul(work[b % 4][:, 0:(R + 1) * HID], cat[0:HID, b * P:(b + 1) * P],
                                  w_rel[k][:].rearrange("i r o -> i (r o)"), start=True, stop=True).then_inc(rel_mm, 1)
                    pe.wait_ge(y_out, NB * (k + 1))
                    pe.wait_ge(root_out, NB * (k + 1))
                for a in range(BANKS):
                    pe.matmul(sums_v[:, a, :], zeros_b[:, 0:P], zeros_b[:], start=True, stop=True)

                def edge_group(i, s, nt, l=l):
                    g = 2 * i + s
                    n = l * NG + g
                    regs = [pe.alloc_register(f"off{l}_{s}_{nt}_{j}") for j in range(GT)]
                    pe.load(regs, offsets[0:1, bass.ds(GT * g, GT)])
                    off = [pe.snap(r, min_val=0, max_val=512 * (BANKS - 1) + REC * (PER_BANK - 1)) for r in regs]
                    pe.wait_ge(onehot_made, done(n))
                    pe.wait_ge(onehot_t_out, reusable(n))
                    for j in range(GT):
                        ins = pe.transpose(turned[s][:, j * P:(j + 1) * P], onehot_b[s][:, j, :], ident_b[:])
                    ins.then_inc(onehot_turned, 1)
                    pe.wait_ge(onehot_t_out, done(n))
                    pe.wait_ge(z_ready, reusable(n))
                    a, w = (0, HID) if l < LAYERS else (HID, R)
                    for j in range(GT):
                        ins = pe.matmul(gathered_ps[s][:, j * w:(j + 1) * w], onehot_t[s][:, j, :],
                                        terms_flat[:, bass.ds(off[j] + a, w)], start=True, stop=True)
                    ins.then_inc(terms_gathered, 1)
                    pe.wait_ge(onehot_out, done(n))
                    pe.wait_ge(msg_ready, done(n))
                    w = REC if l < LAYERS else HID
                    for j in range(GT):
                        ins = pe.matmul(sums[:, bass.ds(off[j], w)], onehot[s][:, j, :], msg[s][:, j, 0:w],
                                        start=False, stop=True, skip_group_check=True)
                    ins.then_inc(summed, 1)
                    for r in regs:
                        pe.free_register(r)

                groups(pe, edge_group)

                if l < LAYERS:
                    pe.wait_ge(mean_ready, l + 1)
                    for c in range(CH):
                        if c >= 2:
                            pe.wait_ge(mean_t_out, CH * l + c - 1)
                        for m, b in enumerate(chunk(c)):
                            ins = pe.transpose(work[c % 2][0:HID + 1, m * P:(m + 1) * P], mean_n[:, b, :], ident[:])
                        ins.then_inc(mean_turned, 1)
                    for c in range(CH):
                        w = P * len(chunk(c))
                        pe.wait_ge(mean_t_out, CH * l + c + 1)
                        if c >= 2:
                            pe.wait_ge(agg_out, CH * l + c - 1)
                        pe.matmul(work[2 + c % 2][:, 0:w], w2e[:], mean_t[:, 512 * c:512 * c + w],
                                  start=True, stop=True).then_inc(agg_mm, 1)
                    for c in range(CH):
                        w = P * len(chunk(c))
                        pe.wait_ge(agg_out, CH * l + c + 1)
                        if c >= 2:
                            pe.wait_ge(hidden_out, CH * l + c - 1)
                        pe.matmul(work[c % 2][0:HID, 0:w], w1n[:], cat[:, 512 * c:512 * c + w],
                                  start=True, stop=True).then_inc(hidden_mm, 1)
                    for c in range(CH):
                        w = P * len(chunk(c))
                        pe.wait_ge(hidden_out, CH * l + c + 1)
                        if c >= 2:
                            pe.wait_ge(state_ready, CH * l + c - 1)
                        pe.matmul(work[2 + c % 2][0:HID, 0:w], w2n[:], hidden[:, 512 * c:512 * c + w],
                                  start=True, stop=True).then_inc(delta_mm, 1)

        @block.vector
        def _(dve):
            steps = [0]

            def step(ins):
                steps[0] += 1
                ins.then_inc(dve_step, 1)
                dve.wait_ge(dve_step, steps[0])

            for t in (xn[:, NB - 1, :], we8[:], w2e[:], no_edge[:]):
                dve.memset(t, 0.0)
            dve.memset(eps[:], EPS)
            dve.memset(zeros_b[:], 0.0)
            dve.memset(ones_e[:], 1.0)
            step(dve.memset(block_step[:], float(REC)))
            for b in range(PER_BANK - 1, NB - 1, PER_BANK):
                dve.memset(block_step[:, b:b + 1], float(512 - REC * (PER_BANK - 1)))
            dve.memset(no_edge[:, :, PLACE:TYPE + 1], -1.0).then_inc(zeroed, 1)
            dve.wait_ge(consts_made, 4)
            dve.tensor_copy(iota_b[:], iota_i[:])
            dve.tensor_copy(iota_r[:], iota_i[:, 0:R])
            dve.tensor_copy(tile_f[:], tile_i[:])
            dve.tensor_copy(ident_b[:], ident[:]).then_inc(consts_cast, 1)
            dve.wait_ge(consts_cast, 1)

            def destination_terms(l):
                for c in range(CH):
                    dve.wait_ge(src_terms_out, CH * l + c + 1)
                    for m, b in enumerate(chunk(c)):
                        at = REC * (b % PER_BANK)
                        ins = dve.tensor_copy(dst_terms[:, b // PER_BANK, at:at + HID],
                                              work[c % 4][:, m * P + HID:(m + 1) * P])
                    ins.then_inc(dst_terms_out, 1)

            destination_terms(0)

            dve.wait_ge(edges_in, 48)
            step(dve.tensor_scalar(part_i, dst_i, 7, None, ALU.logical_shift_right))
            step(dve.tensor_copy(block_f, part_i))
            step(dve.tensor_scalar(part_i, dst_i, P - 1, None, ALU.bitwise_and))
            dve.tensor_copy(meta[:, :, PLACE - HID], part_i)
            dve.tensor_copy(meta[:, :, TYPE - HID], type_i)
            dve.tensor_copy(meta_i[:, :, ROW0 - HID], src_i)
            dve.scalar_tensor_tensor(out=meta_i[:, :, ROW1 - HID], in0=src_i, scalar=float(R), in1=type_i,
                                     op0=ALU.mult, op1=ALU.add)
            for k in range(NB):
                ins = dve.tensor_scalar(in_block[:, k, :], block_f, float(k), None, ALU.is_equal, ALU.add,
                                        accum_out=count[:, k:k + 1])
            ins.then_inc(counted, 1)
            dve.wait_ge(count_mm, 1)
            step(dve.tensor_scalar(tiles_i[:], work[1][:, 0:NB], float(P - 1), None, ALU.add))
            step(dve.tensor_scalar(tiles_i[:], tiles_i[:], 7, None, ALU.logical_shift_right))
            step(dve.tensor_copy(tiles_f[:], tiles_i[:]))
            step(dve.tensor_tensor_scan(tiles_end[:], ones[:, 0:NB], tiles_f[:], 0.0, ALU.mult, ALU.add))
            step(dve.tensor_tensor(first_slot[:], tiles_end[:], tiles_f[:], ALU.subtract))
            step(dve.tensor_scalar(first_slot[:], first_slot[:], float(P), -1.0, ALU.mult, ALU.add))
            step(dve.tensor_tensor(first_slot[0:EP, :], first_slot[0:EP, :], work[0][0:EP, 0:NB], ALU.add))
            assert steps[0] == RANKED
            step(dve.tensor_tensor(passed[:], tile_f[:].unsqueeze(2).to_broadcast([P, GT, NB - 1]),
                                   tiles_end[:, 0:NB - 1].unsqueeze(1).to_broadcast([P, GT, NB - 1]), ALU.is_ge))
            step(dve.tensor_tensor(passed[:], passed[:],
                                   block_step[:].unsqueeze(1).to_broadcast([P, GT, NB - 1]), ALU.mult))
            step(dve.tensor_reduce(off_f[:], passed[:], X_AXIS, ALU.add))
            dve.tensor_copy(off_i[:], off_f[:]).then_inc(off_ready, 1)
            for k in range(NB):
                step(dve.tensor_tensor_scan(rank, ones_e[0:EP, :], in_block[:, k, :], first_slot[0:EP, k:k + 1],
                                            ALU.mult, ALU.add))
                step(dve.copy_predicated(slot_f, in_block[:, k, :].bitcast(U16), rank))
            step(dve.tensor_copy(slot_i, slot_f))
            step(dve.tensor_scalar(addr[:], slot_i, ((1 << 21) - 1) & ~(GT * P - 1), None, ALU.bitwise_and))
            step(dve.tensor_scalar(part_i, slot_i, P - 1, 3, ALU.bitwise_and, ALU.logical_shift_left))
            step(dve.tensor_tensor(addr[:], addr[:], part_i, ALU.bitwise_or))
            step(dve.tensor_scalar(part_i, slot_i, 7, GT - 1, ALU.logical_shift_right, ALU.bitwise_and))
            step(dve.tensor_tensor(addr[:], addr[:], part_i, ALU.bitwise_or))

            def make_records(g, i, s, first):
                dve.wait_ge(term_e_mm, done(g))
                if not first:
                    dve.wait_ge(rec_stored[s], 16 * GT * i)
                dve.tensor_tensor(rec_out[s][:, :, 0:HID],
                                  work[2 + s][0:EP, :].rearrange("p (j f) -> p j f", j=GT),
                                  b1e_all[0:EP, :].unsqueeze(1).to_broadcast([EP, GT, HID]),
                                  ALU.add).then_inc(rec_made, 1)
                dve.tensor_copy(rec_out[s][:, :, HID:REC].bitcast(I32),
                                meta_i[:, bass.ds(GT * g, GT), :]).then_inc(rec_made, 1)
                dve.tensor_copy(addr_out[s][:], addr[:, bass.ds(GT * g, GT)]).then_inc(rec_made, 1)

            dve.sem_inc(rec_made, 6)
            for s in range(2):
                make_records(s, 0, s, True)
            with dve.Fori(1, EG // 2) as i:
                for s in range(2):
                    make_records(2 * i + s, i, s, False)

            for q in (rec_used, onehot_made, z_ready, msg_ready):
                dve.sem_inc(q, 2)

            def norm(t, res):
                step(dve.tensor_reduce(stat[:, 0, :], v, X_AXIS, ALU.add))
                step(dve.tensor_scalar(stat[:, 0, :], stat[:, 0, :], 1.0 / HID, None, ALU.mult))
                step(dve.tensor_tensor(v, v, stat[:, 0, :].unsqueeze(2).to_broadcast([P, NB, HID]), ALU.subtract))
                step(dve.tensor_tensor(res[:], v, v, ALU.mult))
                dve.tensor_reduce(stat[:, 1, :], res[:], X_AXIS, ALU.add).then_inc(var_ready, 1)
                dve.wait_ge(sd_ready, t)
                step(dve.reciprocal(stat[:, 3, :], stat[:, 2, :]))
                dve.tensor_tensor(res[:], v, stat[:, 3, :].unsqueeze(2).to_broadcast([P, NB, HID]),
                                  ALU.mult).then_inc(normed, 1)

            for l in range(2 * LAYERS):
                if 0 < l < LAYERS:
                    destination_terms(l)
                if l >= LAYERS:
                    k = l - LAYERS
                    if k == 0:
                        for c in range(-(-NB // 8)):
                            n = min(8, NB - 8 * c)
                            dve.wait_ge(back_mm, c + 1)
                            dve.tensor_tensor(v[:, 8 * c:8 * c + n, :],
                                              work[c % 2][:, 0:n * HID].rearrange("p (b f) -> p b f", b=n),
                                              xn[:, 8 * c:8 * c + n, :], ALU.add).then_inc(back_out, 1)
                        dve.wait_ge(back_out, -(-NB // 8))
                        norm(1, x1)
                        dve.wait_ge(rel_in, 16 * 3 * LAYERS)
                    for b in range(NB):
                        dve.wait_ge(y_out, NB * k + b + 1)
                        dve.tensor_tensor(root[:, b, :], work[b % 4][:, R * HID:(R + 1) * HID], b_rel[k][:],
                                          ALU.add).then_inc(root_out, 1)

                def edge_group(i, s, nt, l=l):
                    n = l * NG + 2 * i + s
                    rec = rec_in[s]
                    dve.wait_ge(rec_loaded[s], 16 * (l * USES[s] + i + 1))
                    dve.wait_ge(onehot_turned, reusable(n))
                    dve.wait_ge(onehot_out, reusable(n))
                    for j in range(GT):
                        ins = dve.tensor_scalar(onehot_b[s][:, j, :], iota_b[:], rec[:, j, PLACE:PLACE + 1], None,
                                                ALU.is_equal)
                    ins.then_inc(onehot_made, 1)
                    types = rec[:, :, TYPE:TYPE + 1].to_broadcast([P, GT, R])
                    type_row = iota_r[:].unsqueeze(1).to_broadcast([P, GT, R])
                    dve.wait_ge(summed, reusable(n))
                    if l < LAYERS:
                        dve.tensor_tensor(msg[s][:, :, HID:REC], type_row, types, ALU.is_equal)
                        dve.wait_ge(rows_in[s], ROWS_LAYER[s] * l + 16 * GT * i + 16 * nt)
                        dve.wait_ge(msg_ready, reusable(n))
                        dve.tensor_tensor(z[s][:], rows[s][:], rec[:, :, 0:HID], ALU.add).then_inc(rec_used, 1)
                        dve.wait_ge(terms_gathered, done(n))
                        dve.wait_ge(rec_used, done(n))
                        dve.tensor_tensor(z[s][:], z[s][:], gathered_ps[s][:].rearrange("p (j f) -> p j f", j=GT),
                                          ALU.add).then_inc(z_ready, 1)
                    else:
                        m = n - LAYERS * NG
                        dve.tensor_tensor(is_type[s][:], type_row, types, ALU.is_equal).then_inc(share_step, 1)
                        dve.wait_ge(share_step, 3 * m + 1)
                        dve.wait_ge(terms_gathered, done(n))
                        dve.tensor_tensor(is_type[s][:], is_type[s][:],
                                          gathered_ps[s][:, 0:GT * R].rearrange("p (j r) -> p j r", j=GT),
                                          ALU.mult).then_inc(share_step, 1)
                        dve.wait_ge(share_step, 3 * m + 2)
                        dve.tensor_reduce(share[s][:], is_type[s][:], X_AXIS, ALU.add).then_inc(share_step, 1)
                        dve.wait_ge(share_step, 3 * m + 3)
                        dve.sem_inc(z_ready, 1)
                        dve.wait_ge(rows_in[s], ROWS_LAYER[s] * l + 16 * GT * i + 16 * nt)
                        dve.tensor_tensor(msg[s][:, :, 0:HID], rows[s][:],
                                          share[s][:].unsqueeze(2).to_broadcast([P, GT, HID]),
                                          ALU.mult).then_inc(msg_ready, 1)
                        dve.wait_ge(msg_ready, done(n))
                        dve.sem_inc(rec_used, 1)

                groups(dve, edge_group)
                dve.wait_ge(summed, done(l * NG + NG - 1))

                if l < LAYERS:
                    for c in range(BANKS):
                        bs = bank_blocks(c)
                        ins = dve.tensor_reduce(deg[:, 0, bs[0]:bs[-1] + 1], bank_view(sums_v, c, HID, REC),
                                                X_AXIS, ALU.add)
                    step(ins)
                    dve.tensor_scalar(mean_n[:, :, HID], deg[:, 0, :], 1.0, None, ALU.min)
                    step(dve.tensor_scalar(deg[:, 1, :], deg[:, 0, :], 1.0, None, ALU.max))
                    step(dve.reciprocal(deg[:, 2, :], deg[:, 1, :]))
                    for c in range(BANKS):
                        bs = bank_blocks(c)
                        ins = dve.tensor_tensor(mean_n[:, bs[0]:bs[-1] + 1, 0:HID], bank_view(sums_v, c, 0, HID),
                                                deg[:, 2, bs[0]:bs[-1] + 1].unsqueeze(2)
                                                .to_broadcast([P, len(bs), HID]), ALU.mult)
                        if l == LAYERS - 1:
                            ins = dve.tensor_scalar(bank_view(dst_terms, c, HID, REC), bank_view(sums_v, c, HID, REC),
                                                    1.0, None, ALU.max)
                    if l == LAYERS - 1:
                        step(ins)
                        for c in range(BANKS):
                            ins = dve.reciprocal(bank_view(dst_terms, c, HID, REC), bank_view(dst_terms, c, HID, REC))
                    ins.then_inc(mean_ready, 1)
                    for c in range(CH):
                        w = P * len(chunk(c))
                        dve.wait_ge(delta_mm, CH * l + c + 1)
                        at = cat[0:HID, 512 * c:512 * c + w]
                        dve.scalar_tensor_tensor(out=at, in0=work[2 + c % 2][0:HID, 0:w], scalar=b2n_c[:, 0:1],
                                                 in1=at, op0=ALU.add, op1=ALU.add).then_inc(state_ready, 1)
                else:
                    to = v if k == LAYERS - 1 else hn[:]
                    for c in range(BANKS):
                        bs = bank_blocks(c)
                        ins = dve.tensor_tensor(to[:, bs[0]:bs[-1] + 1, :], bank_view(sums_v, c, 0, HID),
                                                root[:, bs[0]:bs[-1] + 1, :], ALU.add)
                    step(ins)
                    if k < LAYERS - 1:
                        dve.tensor_scalar(hn[:], hn[:], 0.0, None, ALU.max).then_inc(layer_out, 1)
                    else:
                        step(dve.tensor_tensor(v, v, x1[:], ALU.add))
                        norm(2, hn)


RANKED = 11


_L0 = ['L0_gnn_' + n for n in ('W1e', 'b1e', 'W2e', 'b2e', 'W1n', 'b1n', 'W2n', 'b2n')]
_INS = ['x', 'src', 'dst', 'edge_attr_16', 'edge_type_4'] + _L0 + [
    f'L1_gnn_{n}{l}' for n in ('W', 'root', 'b') for l in range(3)]


def kernel(**inputs):
    import numpy as _np
    import concourse.bacc as _bacc
    from concourse import mybir as _mybir
    from concourse.bass_utils import run_bass_kernel_spmd as _run

    nc = _bacc.Bacc("TRN2", target_bir_lowering=False, num_devices=1)
    arrays, args = {}, []
    for name in _INS:
        a = _np.ascontiguousarray(inputs[name])
        arrays[f"in_{name}_dram"] = a
        args.append(nc.dram_tensor(f"in_{name}_dram", a.shape, _mybir.dt.from_np(a.dtype), kind="ExternalInput").ap())
    out = nc.dram_tensor("out_0_dram", args[0].shape, _mybir.dt.float32, kind="ExternalOutput").ap()
    gnn_kernel(nc, *args[:13], args[13:16], args[16:19], args[19:22], out)
    r = _run(nc, [arrays], core_ids=[0])
    return r.results[0]["out_0_dram"]
```

```python
from contextlib import ExitStack

import concourse.bass as bass
from concourse import mybir

ALU = mybir.AluOpType
ACT = mybir.ActivationFunctionType
X_AXIS = mybir.AxisListType.X
F32 = mybir.dt.float32
BF16 = mybir.dt.bfloat16
I32 = mybir.dt.int32
U32 = mybir.dt.uint32
I16 = mybir.dt.int16
U16 = mybir.dt.uint16

P = 128
HID = 64
EPS = 1e-5

GT = 8
REC = HID + 4
ROW0, ROW1, PLACE, TYPE = HID, HID + 1, HID + 2, HID + 3
PER_BANK = 512 // REC


def gnn_kernel(nc, x, src, dst, edge_attr, edge_type, W1e, b1e, W2e, b2e, W1n, b1n, W2n, b2n,
               rel_w, rel_root, rel_b, out):
    N = x.shape[0]
    E, ED = edge_attr.shape
    R = rel_w[0].shape[0]
    NB = -(-N // P)
    NP = NB * P
    LAST = N - (NB - 1) * P
    EP = 125
    EC = E // EP
    EG = EC // GT
    TILES = (E + NB * (P - 1)) // P
    NG = -(-TILES // GT)
    QUADS = NG // 4
    GP = GT - 1
    LAST_TILES = TILES - (NG - 1) * GT
    BANKS = -(-NB // PER_BANK)
    CH = -(-NB // 4)
    LAYERS = 3
    assert EP * EC == E and EG % 2 == 0 and NG % 4 == 1 and GT * ED == P and R == 4

    recs = nc.dram_tensor("recs", [NG * GT * P, REC], F32, kind="Internal").ap()
    table0 = nc.dram_tensor("table0", [NP, HID], F32, kind="Internal").ap()
    table1 = nc.dram_tensor("table1", [NP * R, HID], F32, kind="Internal").ap()
    src_rows = nc.dram_tensor("src_rows", [NG, P], I16, kind="Internal").ap()
    recs_by_group = recs.rearrange("(g p j) w -> p g (j w)", p=P, j=GT)
    last_tile_src = recs.rearrange("(g p j) w -> g p j w", p=P, j=GT)[:, :, GT - 1, ROW0:ROW0 + 1]

    def chunk(c):
        return range(4 * c, min(4 * c + 4, NB))

    with ExitStack() as ctx:
        def sb(name, shape, dt=F32):
            return ctx.enter_context(nc.sbuf_tensor(name, shape, dt))

        def ps(name, shape, dt=F32):
            return ctx.enter_context(nc.psum_tensor(name, shape, dt))

        def sem(name):
            return ctx.enter_context(nc.semaphore(name))

        ident = sb("ident", [P, P])
        ident_b = sb("ident_b", [P, P], BF16)
        ones = sb("ones", [P, P])
        before = sb("before", [P, P])
        iota_i = sb("iota_i", [P, P], I32)
        iota_b = sb("iota_b", [P, P], BF16)
        iota_r = sb("iota_r", [P, R])
        tile_i = sb("tile_i", [P, GT], I32)
        node_i = sb("node_i", [P, NB], I32)
        node_grid = sb("node_grid", [P, NB, P], I16)
        tile_f = sb("tile_f", [P, GT])
        block_step = sb("block_step", [P, NB - 1])
        zeros_b = sb("zeros_b", [P, 512], BF16)
        ones_e = sb("ones_e", [P, EC], BF16)
        eps = sb("eps", [P, 1])
        we8 = sb("we8", [P, GT, HID])
        w_ab = sb("w_ab", [HID, 2 * HID])
        b1e_all = sb("b1e_all", [P, HID])
        w2e = sb("w2e", [HID + 1, P])
        w1n = sb("w1n", [P, HID])
        w2n = sb("w2n", [HID, HID])
        b1n_c = sb("b1n_c", [HID, 1])
        b2n_c = sb("b2n_c", [HID, 1])
        w_rel = [sb(f"w_rel{l}", [HID, R + 1, HID]) for l in range(LAYERS)]
        b_rel = [sb(f"b_rel{l}", [P, HID]) for l in range(LAYERS)]
        xn = sb("xn", [P, NB, HID])
        x1 = sb("x1", [P, NB, HID])
        hn = sb("hn", [P, NB, HID])
        cat = sb("cat", [P, NP])
        dst_terms = sb("dst_terms", [P, BANKS, 512])
        terms_flat = dst_terms[:].rearrange("p a b -> p (a b)")
        deg = sb("deg", [P, 4, NB])
        stat = sb("stat", [P, 4, NB])
        arena1 = sb("arena1", [P, 10240])
        arena2 = sb("arena2", [P, 8 * EC + 1664])
        in_block = arena1[0:EP, 0:NB * EC // 2].bitcast(BF16).rearrange("p (k e) -> p k e", k=NB)
        y_rows = arena1[:, 0:NB * R * HID].rearrange("p (b w) -> p b w", b=NB)
        root = arena1[:, NB * R * HID:NB * (R + 1) * HID].rearrange("p (b w) -> p b w", b=NB)
        v = arena1[:, NB * (R + 1) * HID:NB * (R + 2) * HID].rearrange("p (b w) -> p b w", b=NB)

        weight = arena2[:, 0:NG * GT * R].rearrange("p (t r) -> p t r", r=R)

        def edge_row(k, dt=F32):
            return arena2[0:EP, k * EC:(k + 1) * EC].bitcast(dt)

        src_i, dst_i, type_i, part_i = (edge_row(k, I32) for k in range(4))
        block_f, rank, slot_f = (edge_row(k) for k in range(4, 7))
        slot_i = edge_row(7, I32)
        mean_t = arena2[0:HID + 1, 0:NP]
        hidden = arena2[0:HID, NP:2 * NP]
        mean_n = arena2[:, 2 * NP:2 * NP + NB * (HID + 1)].rearrange("p (b w) -> p b w", b=NB)
        arena3 = sb("arena3", [P, 4 * EC])
        meta = arena3[0:EP, :].rearrange("p (e w) -> p e w", w=4)
        meta_i = meta.bitcast(I32)
        src_onehot = [arena3[:, s * NB * P // 2:(s + 1) * NB * P // 2].bitcast(BF16)
                      .rearrange("p (b e) -> p b e", b=NB) for s in range(2)]
        arena4 = sb("arena4", [P, NB * 3 * HID // 2])
        addr = arena4[0:EP, 0:EC].bitcast(I32)
        src_split = arena4[:].bitcast(BF16).rearrange("p (b k f) -> p b k f", b=NB, k=3)
        count = sb("count", [EP, NB])
        tiles_i = sb("tiles_i", [P, NB], I32)
        tiles_f = sb("tiles_f", [P, NB])
        tiles_end = sb("tiles_end", [P, NB])
        first_slot = sb("first_slot", [P, NB])
        passed = sb("passed", [P, GT, NB - 1])
        off_f = sb("off_f", [P, GT])
        off_i = sb("off_i", [P, GT], I32)
        offsets = sb("offsets", [1, NG * GT], I32)
        ea = [sb(f"ea{s}", [EP, P]) for s in range(2)]
        ea_t = [sb(f"ea_t{s}", [P, EP]) for s in range(2)]
        addr_out = [sb(f"addr_out{s}", [EP, GT], I32) for s in range(2)]
        rec_in = [sb(f"rec_in{s}", [P, GT, REC]) for s in range(4)]
        src_in = [sb(f"src_in{s}", [P, P], I16) for s in range(4)]
        src_cols = sb("src_cols", [NG, P], I32)
        src_cols16 = sb("src_cols16", [NG, P], I16)
        rows = [sb(f"rows{s}", [P, GP, HID]) for s in range(2)]
        src_row = [sb(f"src_row{s}", [P, 2 * HID]) for s in range(2)]
        src_t = [sb(f"src_t{s}", [HID, P]) for s in range(2)]
        by_type = [sb(f"by_type{s}", [P, R, HID]) for s in range(2)]
        onehot_b = [sb(f"onehot_b{s}", [P, GT, P], BF16) for s in range(2)]
        onehot = [sb(f"onehot{s}", [P, GT, P]) for s in range(2)]
        onehot_t = [sb(f"onehot_t{s}", [P, GT, P]) for s in range(2)]
        z = [sb(f"z{s}", [P, GT, HID]) for s in range(2)]
        msg = [sb(f"msg{s}", [P, GT, REC]) for s in range(2)]
        rec_out = [msg[s][0:EP, :, :] for s in range(2)]
        no_edge = rec_in[3]
        is_type = [sb(f"is_type{s}", [P, GT, R]) for s in range(2)]
        share = [sb(f"share{s}", [P, GT]) for s in range(2)]

        sums = ps("sums", [P, BANKS * 512])
        sums_v = sums[:].rearrange("p (a b) -> p a b", a=BANKS)
        work = [ps(f"work{k}", [P, 512]) for k in range(4)]
        turned = work[0][:].bitcast(BF16)
        src_ps = work[1]
        gathered_ps = [work[2 + s] for s in range(2)]

        def bank_blocks(c):
            return range(PER_BANK * c, min(PER_BANK * c + PER_BANK, NB))

        def bank_view(t, c, a, b):
            n = len(bank_blocks(c))
            return t[:, c, 0:n * REC].rearrange("p (i w) -> p i w", w=REC)[:, :, a:b]

        pool_step = sem("pool_step")
        consts_made = sem("consts_made")
        consts_cast = sem("consts_cast")
        weights_in = sem("weights_in")
        zeroed = sem("zeroed")
        rel_in = sem("rel_in")
        x_in = sem("x_in")
        edges_in = sem("edges_in")
        recs_blank = sem("recs_blank")
        dve_step = sem("dve_step")
        turn_mm = sem("turn_mm")
        turn_out = sem("turn_out")
        term_mm = sem("term_mm")
        src_terms_out = sem("src_terms_out")
        dst_terms_out = sem("dst_terms_out")
        table_stored = sem("table_stored")
        mean_ready = sem("mean_ready")
        mean_turned = sem("mean_turned")
        mean_t_out = sem("mean_t_out")
        agg_mm = sem("agg_mm")
        agg_out = sem("agg_out")
        hidden_mm = sem("hidden_mm")
        hidden_out = sem("hidden_out")
        delta_mm = sem("delta_mm")
        state_ready = sem("state_ready")
        back_mm = sem("back_mm")
        back_out = sem("back_out")
        var_ready = sem("var_ready")
        sd_ready = sem("sd_ready")
        normed = sem("normed")
        rel_mm = sem("rel_mm")
        y_out = sem("y_out")
        root_out = sem("root_out")
        layer_out = sem("layer_out")
        stored = sem("stored")
        counted = sem("counted")
        count_mm = sem("count_mm")
        off_ready = sem("off_ready")
        offsets_in = sem("offsets_in")
        ea_in = [sem(f"ea_in{s}") for s in range(2)]
        ea_turned = sem("ea_turned")
        ea_t_out = sem("ea_t_out")
        term_e_mm = sem("term_e_mm")
        rec_made = sem("rec_made")
        scatter_go = sem("scatter_go")
        rec_stored = [sem(f"rec_stored{s}") for s in range(2)]
        rec_loaded = [sem(f"rec_loaded{s}") for s in range(4)]
        rec_used = sem("rec_used")
        split_step = sem("split_step")
        split_ready = sem("split_ready")
        src_cols_in = sem("src_cols_in")
        src_rows_stored = sem("src_rows_stored")
        src_onehot_made = sem("src_onehot_made")
        src_gathered = sem("src_gathered")
        src_out = sem("src_out")
        src_cols_cast = sem("src_cols_cast")
        src_turned = sem("src_turned")
        src_t_out = sem("src_t_out")
        gather_go = sem("gather_go")
        rows_in = [sem(f"rows_in{s}") for s in range(2)]
        onehot_made = sem("onehot_made")
        onehot_turned = sem("onehot_turned")
        onehot_out = sem("onehot_out")
        onehot_t_out = sem("onehot_t_out")
        terms_gathered = sem("terms_gathered")
        z_ready = sem("z_ready")
        msg_ready = sem("msg_ready")
        summed = sem("summed")
        share_step = sem("share_step")

        def done(n, start=2):
            return n + 1 + start

        def reusable(n):
            return n + 1

        RECS = 4
        USES = [QUADS + 1, QUADS, QUADS, QUADS]
        ROWS_LAYER = [16 * (GP * 2 * QUADS + LAST_TILES), 16 * GP * 2 * QUADS]

        def rows_landed(l, i, u, nt):
            return ROWS_LAYER[u % 2] * l + 16 * GP * (2 * i + u // 2) + 16 * nt

        def groups(eng, body):
            with eng.Fori(0, QUADS) as i:
                for u in range(4):
                    body(i, u, GP)
            body(QUADS, 0, LAST_TILES)

        def staged_groups(eng, ahead, body, body_first=False, before=None):
            ahead(0, 0)
            with eng.Fori(0, QUADS) as i:
                for u in range(4):
                    if before:
                        before(i, u)
                    if body_first:
                        body(i, u, GP)
                    ahead(i + (u + 1) // 4, (u + 1) % 4)
                    if not body_first:
                        body(i, u, GP)
            if before:
                before(QUADS, 0)
            body(QUADS, 0, LAST_TILES)

        block = ctx.enter_context(nc.Block())

        @block.sync
        def _(sp):
            for t, a in ((dst_i, dst), (src_i, src), (type_i, edge_type)):
                sp.dma_start(t, a.rearrange("(p e) -> p e", p=EP)).then_inc(edges_in, 16)
            sp.wait_ge(zeroed, 1)
            sp.dma_start(xn[:, 0:NB - 1, :],
                         x[0:(NB - 1) * P, :].rearrange("(b p) f -> p b f", p=P)).then_inc(x_in, 16)
            sp.dma_start(xn[0:LAST, NB - 1, :], x[(NB - 1) * P:N, :]).then_inc(x_in, 16)

            attr = edge_attr.rearrange("(p e) f -> p (e f)", p=EP)

            def load_attr(g, s):
                sp.wait_ge(ea_turned, g + 1)
                sp.dma_start(ea[s][:], attr[:, bass.ds(g * P, P)]).then_inc(ea_in[s], 16)

            def store_table0(l):
                sp.wait_ge(src_terms_out, CH * (l + 1))
                sp.dma_start(table0.rearrange("(b p) f -> p b f", p=P), hn[:]).then_inc(table_stored, 16)

            store_table0(0)
            sp.wait_ge(off_ready, 1)
            sp.dma_start(offsets[0:1, :], off_i[0:NG, :]).then_inc(offsets_in, 16)
            with sp.Fori(0, EG // 2) as i:
                for s in range(2):
                    load_attr(2 * i + s, s)
            for s in range(2):
                sp.wait_ge(rec_stored[s], 16 * GT * (EG // 2))

            sp.dma_start(src_cols[:].bitcast(F32).unsqueeze(2), last_tile_src,
                         allow_slow_non_contiguous=True).then_inc(src_cols_in, 16)
            sp.wait_ge(src_cols_cast, 1)
            sp.dma_start(src_rows, src_cols16[:]).then_inc(src_rows_stored, 16)
            sp.wait_ge(src_rows_stored, 16)

            for l in range(2 * LAYERS):
                if 0 < l < LAYERS:
                    store_table0(l)
                if l >= LAYERS:
                    k = l - LAYERS
                    sp.wait_ge(y_out, NB * (k + 1))
                    sp.dma_start(table1.rearrange("(b p r) f -> p b (r f)", p=P, r=R),
                                 y_rows).then_inc(table_stored, 16)

                def load_group(i, u, nt, l=l):
                    g = 4 * i + u
                    sp.wait_ge(rec_used, done(l * NG + g - 4, RECS))
                    sp.dma_start(rec_in[u][:].rearrange("p j w -> p (j w)"),
                                 recs_by_group[:, bass.ds(g, 1), :].rearrange("p a w -> p (a w)")
                                 ).then_inc(rec_loaded[u], 16)
                    sp.dma_start(src_in[u][:], src_rows[bass.ds(g, 1), :].to_broadcast([P, P])
                                 ).then_inc(rec_loaded[u], 16)

                groups(sp, load_group)
            sp.wait_ge(normed, 2)
            sp.dma_start(out[0:(NB - 1) * P, :].rearrange("(b p) f -> p b f", p=P),
                         hn[:, 0:NB - 1, :]).then_inc(stored, 16)
            sp.dma_start(out[(NB - 1) * P:N, :], hn[0:LAST, NB - 1, :]).then_inc(stored, 16)
            sp.wait_ge(stored, 32)

        @block.gpsimd
        def _(pool):
            pool.memset(ident[:], 0.0).then_inc(pool_step, 1)
            pool.memset(ones[:], 1.0).then_inc(pool_step, 1)
            pool.iota(iota_i[:], [[1, P]], base=0, channel_multiplier=0).then_inc(consts_made, 1)
            pool.iota(tile_i[:], [[1, GT]], base=0, channel_multiplier=GT).then_inc(consts_made, 1)
            pool.iota(node_i[:], [[P, NB]], base=0, channel_multiplier=1).then_inc(consts_made, 1)
            pool.wait_ge(pool_step, 2)
            pool.affine_select(out=ident[:], in_=ident[:], compare_op=ALU.not_equal, fill=1.0,
                               base=0, pattern=[[-1, P]], channel_multiplier=1).then_inc(consts_made, 1)
            pool.affine_select(out=before[:], in_=ones[:], compare_op=ALU.is_gt, fill=0.0,
                               base=0, pattern=[[1, P]], channel_multiplier=-1).then_inc(consts_made, 1)

            pool.wait_ge(recs_blank, 16)
            with pool.Fori(0, EG // 2) as i:
                for s in range(2):
                    pool.wait_ge(rec_made, 3 * (2 * i + s) + 9)
                    pool.sem_inc(scatter_go, 1)
                    for j in range(GT):
                        pool.indirect_dma_start(
                            recs, bass.IndirectOffsetOnAxis(ap=addr_out[s][:, j:j + 1].bitcast(U32), axis=0),
                            rec_out[s][:, j, :], None).then_inc(rec_stored[s], 16)

            for l in range(2 * LAYERS):
                pool.wait_ge(table_stored, 16 * (l + 1))
                table = table0 if l < LAYERS else table1
                field = ROW0 if l < LAYERS else ROW1

                def gather(i, u, nt, l=l):
                    n = l * NG + 4 * i + u
                    s = u % 2
                    pool.wait_ge(rec_used, done(n - 2, RECS))
                    pool.wait_ge(rec_loaded[u], 32 * (l * USES[u] + i + 1))
                    pool.sem_inc(gather_go, 1)
                    for j in range(nt):
                        pool.indirect_dma_start(
                            rows[s][:, j, :], None, table,
                            bass.IndirectOffsetOnAxis(ap=rec_in[u][:, j, field:field + 1].bitcast(U32), axis=0)
                        ).then_inc(rows_in[s], 16)

                groups(pool, gather)

        @block.scalar
        def _(act):
            act.wait_ge(zeroed, 1)
            for i in range(GT):
                act.dma_start(we8[ED * i:ED * (i + 1), i, :], W1e[2 * HID:2 * HID + ED, :]).then_inc(weights_in, 16)
            act.dma_start(w_ab[:, 0:HID], W1e[0:HID, :]).then_inc(weights_in, 16)
            act.dma_start(w_ab[:, HID:2 * HID], W1e[HID:2 * HID, :]).then_inc(weights_in, 16)
            act.dma_start(b1e_all[:], b1e.partition_broadcast(P)).then_inc(weights_in, 16)
            act.dma_start(w2e[0:HID, HID:P], W2e).then_inc(weights_in, 16)
            act.dma_start(w2e[HID:HID + 1, HID:P], b2e.rearrange("(a f) -> a f", a=1)).then_inc(weights_in, 16)
            act.dma_start(w1n[:], W1n).then_inc(weights_in, 16)
            act.dma_start(w2n[:], W2n).then_inc(weights_in, 16)
            act.dma_start(b1n_c[:], b1n.rearrange("(f a) -> f a", a=1)).then_inc(weights_in, 16)
            act.dma_start(b2n_c[:], b2n.rearrange("(f a) -> f a", a=1)).then_inc(weights_in, 16)
            act.dma_start(recs_by_group, no_edge[:].rearrange("p j w -> p (j w)").unsqueeze(1)
                          .to_broadcast([P, NG, GT * REC])).then_inc(recs_blank, 16)
            for l in range(LAYERS):
                act.dma_start(w_rel[l][:, 0:R, :], rel_w[l].rearrange("r i o -> i r o")).then_inc(rel_in, 16)
                act.dma_start(w_rel[l][:, R, :], rel_root[l]).then_inc(rel_in, 16)
                act.dma_start(b_rel[l][:], rel_b[l].partition_broadcast(P)).then_inc(rel_in, 16)

            def turn_state(t):
                for c in range(CH):
                    w = P * len(chunk(c))
                    act.wait_ge(turn_mm, CH * t + c + 1)
                    act.copy(cat[0:HID, 512 * c:512 * c + w], work[c % 2][0:HID, 0:w]).then_inc(turn_out, 1)

            def source_terms(l):
                for c in range(CH):
                    n = len(chunk(c))
                    act.wait_ge(term_mm, CH * l + c + 1)
                    act.copy(hn[:, 4 * c:4 * c + n, :],
                             work[c % 4][:, 0:P * n].rearrange("p (b w) -> p b w", b=n)[:, :, 0:HID]
                             ).then_inc(src_terms_out, 1)

            turn_state(0)
            source_terms(0)

            for q in (ea_t_out, onehot_out, onehot_t_out):
                act.sem_inc(q, 2)
            with act.Fori(0, EG // 2) as i:
                for s in range(2):
                    g = 2 * i + s
                    act.wait_ge(ea_turned, done(g))
                    act.wait_ge(term_e_mm, reusable(g))
                    act.copy(ea_t[s][:], work[s][:, 0:EP]).then_inc(ea_t_out, 1)

            for l in range(2 * LAYERS):
                if 0 < l < LAYERS:
                    source_terms(l)
                if l >= LAYERS:
                    k = l - LAYERS
                    if k == 0:
                        act.wait_ge(var_ready, 1)
                        act.activation(stat[:, 2, :], stat[:, 1, :], ACT.Sqrt, bias=eps[:, 0:1],
                                       scale=1.0 / HID).then_inc(sd_ready, 1)
                    turn_state(1 + k)
                    for b in range(NB):
                        act.wait_ge(rel_mm, NB * k + b + 1)
                        act.copy(y_rows[:, b, :], work[b % 4][:, 0:R * HID]).then_inc(y_out, 1)

                def one_hots(i, u, l=l):
                    n = l * NG + 4 * i + u
                    s = u % 2
                    if l <= LAYERS:
                        act.wait_ge(onehot_turned, done(n))
                        act.wait_ge(terms_gathered, reusable(n))
                        act.copy(onehot_t[s][:].rearrange("p j n -> p (j n)"), turned).then_inc(onehot_t_out, 1)
                    act.wait_ge(onehot_made, done(n))
                    act.wait_ge(summed, reusable(n))
                    act.copy(onehot[s][:], onehot_b[s][:]).then_inc(onehot_out, 1)

                def messages(i, u, nt, l=l):
                    n = l * NG + 4 * i + u
                    s = u % 2
                    if l >= LAYERS:
                        m = n - LAYERS * NG
                        act.wait_ge(src_turned, m + 1)
                        act.wait_ge(terms_gathered, reusable(n))
                        act.copy(src_t[s][:], gathered_ps[s][0:HID, HID:HID + P]).then_inc(src_t_out, 1)
                    if l < LAYERS:
                        act.wait_ge(z_ready, done(n))
                        act.activation(msg[s][:, :, 0:HID], z[s][:], ACT.Silu).then_inc(msg_ready, 1)

                staged_groups(act, one_hots, messages, body_first=l >= LAYERS)

                if l < LAYERS:
                    for c in range(CH):
                        w = P * len(chunk(c))
                        act.wait_ge(mean_turned, CH * l + c + 1)
                        act.copy(mean_t[:, 512 * c:512 * c + w], work[c % 2][0:HID + 1, 0:w]).then_inc(mean_t_out, 1)
                    for c in range(CH):
                        w = P * len(chunk(c))
                        act.wait_ge(agg_mm, CH * l + c + 1)
                        act.copy(cat[HID:P, 512 * c:512 * c + w], work[2 + c % 2][HID:P, 0:w]).then_inc(agg_out, 1)
                    for c in range(CH):
                        w = P * len(chunk(c))
                        act.wait_ge(hidden_mm, CH * l + c + 1)
                        act.activation(hidden[:, 512 * c:512 * c + w], work[c % 2][0:HID, 0:w], ACT.Silu,
                                       bias=b1n_c[:, 0:1]).then_inc(hidden_out, 1)
            act.wait_ge(var_ready, 2)
            act.activation(stat[:, 2, :], stat[:, 1, :], ACT.Sqrt, bias=eps[:, 0:1],
                           scale=1.0 / HID).then_inc(sd_ready, 1)

        @block.tensor
        def _(pe):
            pe.wait_ge(consts_made, 5)
            pe.wait_ge(x_in, 32)

            loads = [0]

            def turn_state(t, nodes):
                for c in range(CH):
                    if c >= 2:
                        pe.wait_ge(turn_out, CH * t + c - 1)
                    for m, b in enumerate(chunk(c)):
                        ins = pe.transpose(work[c % 2][0:HID, m * P:(m + 1) * P], nodes[:, b, :], ident[:])
                    ins.then_inc(turn_mm, 1)

            def terms(l):
                for c in range(CH):
                    if c >= 4:
                        pe.wait_ge(src_terms_out, CH * l + c - 3)
                        pe.wait_ge(dst_terms_out, CH * l + c - 3)
                    for m, b in enumerate(chunk(c)):
                        ins = pe.matmul(work[c % 4][:, m * P:(m + 1) * P], cat[0:HID, b * P:(b + 1) * P],
                                        w_ab[:], start=True, stop=True)
                    ins.then_inc(term_mm, 1)

            turn_state(0, xn)
            pe.wait_ge(turn_out, CH)

            pe.wait_ge(counted, 1)
            pe.matmul(work[0][0:EP, 0:NB], before[0:EP, 0:EP], count[:], start=True, stop=True)
            pe.matmul(work[1][:, 0:NB], ones[0:EP, :], count[:], start=True, stop=True).then_inc(count_mm, 1)
            pe.wait_ge(dve_step, RANKED)
            pe.wait_ge(weights_in, 16 * (GT + 9))
            terms(0)
            pe.wait_ge(src_terms_out, CH)
            pe.wait_ge(dst_terms_out, CH)
            for q in (ea_turned, term_e_mm, onehot_turned, src_gathered, terms_gathered, summed):
                pe.sem_inc(q, 2)
            with pe.Fori(0, EG // 2) as i:
                for s in range(2):
                    g = 2 * i + s
                    pe.wait_ge(ea_in[s], 16 * (i + 1))
                    pe.wait_ge(ea_t_out, reusable(g))
                    pe.transpose(work[s][:, 0:EP], ea[s][:], ident[0:EP, 0:EP]).then_inc(ea_turned, 1)
                    pe.wait_ge(ea_t_out, done(g))
                    pe.wait_ge(rec_made, 3 * g + 1)
                    pe.matmul(work[2 + s][0:EP, :], ea_t[s][:], we8[:].rearrange("p i f -> p (i f)"),
                              start=True, stop=True).then_inc(term_e_mm, 1)

            pe.wait_ge(offsets_in, 16)
            pe.wait_ge(consts_cast, 1)
            pe.wait_ge(rec_made, 3 * EG + 6)
            for l in range(2 * LAYERS):
                if 0 < l < LAYERS:
                    pe.wait_ge(state_ready, CH * l)
                    terms(l)
                if l < LAYERS:
                    pe.wait_ge(src_terms_out, CH * (l + 1))
                    pe.wait_ge(dst_terms_out, CH * (l + 1))
                if l >= LAYERS:
                    k = l - LAYERS
                    if k == 0:
                        pe.wait_ge(rel_in, 16 * 3 * LAYERS)
                        pe.wait_ge(state_ready, CH * LAYERS)
                        for c in range(-(-NB // 8)):
                            if c >= 2:
                                pe.wait_ge(back_out, c - 1)
                            for m, b in enumerate(range(8 * c, min(8 * c + 8, NB))):
                                ins = pe.transpose(work[c % 2][:, m * HID:(m + 1) * HID],
                                                   cat[0:HID, b * P:(b + 1) * P], ident[0:HID, 0:HID])
                            ins.then_inc(back_mm, 1)
                        pe.wait_ge(normed, 1)
                    else:
                        pe.wait_ge(layer_out, k)
                    turn_state(1 + k, x1 if k == 0 else hn)
                    pe.wait_ge(turn_out, CH * (2 + k))
                    for b in range(NB):
                        if b >= 4:
                            pe.wait_ge(y_out, NB * k + b - 3)
                            pe.wait_ge(root_out, NB * k + b - 3)
                        pe.matmul(work[b % 4][:, 0:(R + 1) * HID], cat[0:HID, b * P:(b + 1) * P],
                                  w_rel[k][:].rearrange("i r o -> i (r o)"), start=True, stop=True).then_inc(rel_mm, 1)
                    pe.wait_ge(y_out, NB * (k + 1))
                    pe.wait_ge(root_out, NB * (k + 1))
                pe.wait_ge(split_ready, l + 1)
                for a in range(BANKS):
                    pe.matmul(sums_v[:, a, :], zeros_b[:, 0:P], zeros_b[:], start=True, stop=True)

                def turn_one_hots(g, u, l=l):
                    n = l * NG + g
                    s = u % 2
                    if l > LAYERS:
                        return
                    pe.wait_ge(onehot_made, done(n))
                    pe.wait_ge(onehot_t_out, done(n - 1))
                    for j in range(GT):
                        ins = pe.transpose(turned[:, j * P:(j + 1) * P], onehot_b[s][:, j, :], ident_b[:])
                    ins.then_inc(onehot_turned, 1)

                def gather_sources(g, u, l=l):
                    n = l * NG + g
                    s = u % 2
                    pe.wait_ge(src_onehot_made, done(n))
                    pe.wait_ge(src_out, done(n - 1))
                    for b in range(NB):
                        ins = pe.matmul(src_ps[:, 0:3 * HID], src_onehot[s][:, b, :],
                                        src_split[:, b, :, :].rearrange("p k f -> p (k f)"),
                                        start=(b == 0), stop=(b == NB - 1))
                    ins.then_inc(src_gathered, 1)

                def tile_offsets(g):
                    loads[0] += 1
                    regs = [pe.alloc_register(f"off{loads[0]}_{j}") for j in range(GT)]
                    pe.load(regs, offsets[0:1, bass.ds(GT * g, GT)])
                    return regs, [pe.snap(r, min_val=0, max_val=512 * (BANKS - 1) + REC * (PER_BANK - 1))
                                  for r in regs]

                def gather_terms(g, u, l=l):
                    n = l * NG + g
                    s = u % 2
                    if l <= LAYERS:
                        regs, off = tile_offsets(g)
                    pe.wait_ge(z_ready, reusable(n))
                    if l <= LAYERS:
                        pe.wait_ge(onehot_t_out, done(n))
                        a, w = (0, HID) if l < LAYERS else (HID, R)
                        for j in range(GT):
                            ins = pe.matmul(gathered_ps[s][:, j * w:(j + 1) * w], onehot_t[s][:, j, :],
                                            terms_flat[:, bass.ds(off[j] + a, w)], start=True, stop=True)
                        for r in regs:
                            pe.free_register(r)
                    if l < LAYERS:
                        ins.then_inc(terms_gathered, 1)
                    else:
                        pe.wait_ge(src_out, done(n))
                        pe.transpose(gathered_ps[s][:, HID:HID + P], src_row[s][:], ident[:]).then_inc(src_turned, 1)

                def relate(g, u, l=l):
                    n = l * NG + g
                    s = u % 2
                    pe.wait_ge(src_t_out, n - LAYERS * NG + 1)
                    pe.matmul(gathered_ps[s][:, R * HID:2 * R * HID], src_t[s][:],
                              w_rel[l - LAYERS][:, 0:R, :].rearrange("i r o -> i (r o)"),
                              start=True, stop=True).then_inc(terms_gathered, 1)

                def add_up(g, u, l=l):
                    n = l * NG + g
                    s = u % 2
                    regs, off = tile_offsets(g)
                    pe.wait_ge(onehot_out, done(n))
                    pe.wait_ge(msg_ready, done(n))
                    w = REC if l < LAYERS else HID
                    for j in range(GT):
                        ins = pe.matmul(sums[:, bass.ds(off[j], w)], onehot[s][:, j, :], msg[s][:, j, 0:w],
                                        start=False, stop=True, skip_group_check=True)
                    ins.then_inc(summed, 1)
                    for r in regs:
                        pe.free_register(r)

                def stage(g, u, l=l):
                    gather_sources(g, u)
                    peeled = isinstance(g, int)
                    if l < LAYERS:
                        gather_terms(g, u)
                        if not peeled or g < NG - 1:
                            turn_one_hots(g + 1, (u + 1) % 4)
                        if not peeled or g > 0:
                            add_up(g - 1, (u - 1) % 4)
                    else:
                        if not peeled or g > 0:
                            add_up(g - 1, (u - 1) % 4)
                        gather_terms(g, u)
                        if not peeled or g < NG - 1:
                            turn_one_hots(g + 1, (u + 1) % 4)
                        relate(g, u)

                turn_one_hots(0, 0)
                stage(0, 0)
                with pe.Fori(0, QUADS - 1) as i:
                    for u in range(1, 5):
                        stage(4 * i + u, u % 4)
                for g in range(NG - 4, NG):
                    stage(g, g % 4)
                add_up(NG - 1, (NG - 1) % 4)

                if l < LAYERS:
                    pe.wait_ge(mean_ready, l + 1)
                    for c in range(CH):
                        if c >= 2:
                            pe.wait_ge(mean_t_out, CH * l + c - 1)
                        for m, b in enumerate(chunk(c)):
                            ins = pe.transpose(work[c % 2][0:HID + 1, m * P:(m + 1) * P], mean_n[:, b, :], ident[:])
                        ins.then_inc(mean_turned, 1)
                    for c in range(CH):
                        w = P * len(chunk(c))
                        pe.wait_ge(mean_t_out, CH * l + c + 1)
                        if c >= 2:
                            pe.wait_ge(agg_out, CH * l + c - 1)
                        pe.matmul(work[2 + c % 2][:, 0:w], w2e[:], mean_t[:, 512 * c:512 * c + w],
                                  start=True, stop=True).then_inc(agg_mm, 1)
                    for c in range(CH):
                        w = P * len(chunk(c))
                        pe.wait_ge(agg_out, CH * l + c + 1)
                        if c >= 2:
                            pe.wait_ge(hidden_out, CH * l + c - 1)
                        pe.matmul(work[c % 2][0:HID, 0:w], w1n[:], cat[:, 512 * c:512 * c + w],
                                  start=True, stop=True).then_inc(hidden_mm, 1)
                    for c in range(CH):
                        w = P * len(chunk(c))
                        pe.wait_ge(hidden_out, CH * l + c + 1)
                        if c >= 2:
                            pe.wait_ge(state_ready, CH * l + c - 1)
                        pe.matmul(work[2 + c % 2][0:HID, 0:w], w2n[:], hidden[:, 512 * c:512 * c + w],
                                  start=True, stop=True).then_inc(delta_mm, 1)

        @block.vector
        def _(dve):
            steps = [0]

            def step(ins):
                steps[0] += 1
                ins.then_inc(dve_step, 1)
                dve.wait_ge(dve_step, steps[0])

            for t in (xn[:, NB - 1, :], we8[:], w2e[:], no_edge[:], src_row[0][:], src_row[1][:]):
                dve.memset(t, 0.0)
            dve.memset(eps[:], EPS)
            dve.memset(zeros_b[:], 0.0)
            dve.memset(ones_e[:], 1.0)
            step(dve.memset(block_step[:], float(REC)))
            for b in range(PER_BANK - 1, NB - 1, PER_BANK):
                dve.memset(block_step[:, b:b + 1], float(512 - REC * (PER_BANK - 1)))
            dve.memset(no_edge[:, :, PLACE:TYPE + 1], -1.0).then_inc(zeroed, 1)
            dve.wait_ge(consts_made, 5)
            dve.tensor_copy(iota_b[:], iota_i[:])
            dve.tensor_copy(iota_r[:], iota_i[:, 0:R])
            dve.tensor_copy(tile_f[:], tile_i[:])
            dve.tensor_copy(node_grid[:], node_i[:].unsqueeze(2).to_broadcast([P, NB, P]))
            dve.tensor_copy(ident_b[:], ident[:]).then_inc(consts_cast, 1)
            dve.wait_ge(consts_cast, 1)

            def destination_terms(l):
                for c in range(CH):
                    dve.wait_ge(src_terms_out, CH * l + c + 1)
                    for m, b in enumerate(chunk(c)):
                        at = REC * (b % PER_BANK)
                        ins = dve.tensor_copy(dst_terms[:, b // PER_BANK, at:at + HID],
                                              work[c % 4][:, m * P + HID:(m + 1) * P])
                    ins.then_inc(dst_terms_out, 1)

            dve.wait_ge(edges_in, 48)
            step(dve.tensor_scalar(part_i, dst_i, 7, None, ALU.logical_shift_right))
            step(dve.tensor_copy(block_f, part_i))
            step(dve.tensor_scalar(part_i, dst_i, P - 1, None, ALU.bitwise_and))
            dve.tensor_copy(meta[:, :, PLACE - HID], part_i)
            dve.tensor_copy(meta[:, :, TYPE - HID], type_i)
            dve.tensor_copy(meta_i[:, :, ROW0 - HID], src_i)
            dve.scalar_tensor_tensor(out=meta_i[:, :, ROW1 - HID], in0=src_i, scalar=float(R), in1=type_i,
                                     op0=ALU.mult, op1=ALU.add)
            for k in range(NB):
                ins = dve.tensor_scalar(in_block[:, k, :], block_f, float(k), None, ALU.is_equal, ALU.add,
                                        accum_out=count[:, k:k + 1])
            ins.then_inc(counted, 1)
            dve.wait_ge(count_mm, 1)
            step(dve.tensor_scalar(tiles_i[:], work[1][:, 0:NB], float(P - 1), None, ALU.add))
            step(dve.tensor_scalar(tiles_i[:], tiles_i[:], 7, None, ALU.logical_shift_right))
            step(dve.tensor_copy(tiles_f[:], tiles_i[:]))
            step(dve.tensor_tensor_scan(tiles_end[:], ones[:, 0:NB], tiles_f[:], 0.0, ALU.mult, ALU.add))
            step(dve.tensor_tensor(first_slot[:], tiles_end[:], tiles_f[:], ALU.subtract))
            step(dve.tensor_scalar(first_slot[:], first_slot[:], float(P), -1.0, ALU.mult, ALU.add))
            step(dve.tensor_tensor(first_slot[0:EP, :], first_slot[0:EP, :], work[0][0:EP, 0:NB], ALU.add))
            assert steps[0] == RANKED
            step(dve.tensor_tensor(passed[:], tile_f[:].unsqueeze(2).to_broadcast([P, GT, NB - 1]),
                                   tiles_end[:, 0:NB - 1].unsqueeze(1).to_broadcast([P, GT, NB - 1]), ALU.is_ge))
            step(dve.tensor_tensor(passed[:], passed[:],
                                   block_step[:].unsqueeze(1).to_broadcast([P, GT, NB - 1]), ALU.mult))
            step(dve.tensor_reduce(off_f[:], passed[:], X_AXIS, ALU.add))
            dve.tensor_copy(off_i[:], off_f[:]).then_inc(off_ready, 1)
            for k in range(NB):
                if k == NB // 2:
                    destination_terms(0)
                step(dve.tensor_tensor_scan(rank, ones_e[0:EP, :], in_block[:, k, :], first_slot[0:EP, k:k + 1],
                                            ALU.mult, ALU.add))
                step(dve.copy_predicated(slot_f, in_block[:, k, :].bitcast(U16), rank))
            step(dve.tensor_copy(slot_i, slot_f))
            step(dve.tensor_scalar(addr, slot_i, ((1 << 21) - 1) & ~(GT * P - 1), None, ALU.bitwise_and))
            step(dve.tensor_scalar(part_i, slot_i, P - 1, 3, ALU.bitwise_and, ALU.logical_shift_left))
            step(dve.tensor_tensor(addr, addr, part_i, ALU.bitwise_or))
            step(dve.tensor_scalar(part_i, slot_i, 7, GT - 1, ALU.logical_shift_right, ALU.bitwise_and))
            step(dve.tensor_tensor(addr, addr, part_i, ALU.bitwise_or))

            def make_records(g, i, s, first):
                dve.wait_ge(term_e_mm, done(g))
                if not first:
                    dve.wait_ge(rec_stored[s], 16 * GT * i)
                dve.tensor_tensor(rec_out[s][:, :, 0:HID],
                                  work[2 + s][0:EP, :].rearrange("p (j f) -> p j f", j=GT),
                                  b1e_all[0:EP, :].unsqueeze(1).to_broadcast([EP, GT, HID]),
                                  ALU.add).then_inc(rec_made, 1)
                dve.tensor_copy(rec_out[s][:, :, HID:REC].bitcast(I32),
                                meta_i[:, bass.ds(GT * g, GT), :]).then_inc(rec_made, 1)
                dve.tensor_copy(addr_out[s][:], addr[:, bass.ds(GT * g, GT)]).then_inc(rec_made, 1)

            dve.sem_inc(rec_made, 6)
            for s in range(2):
                make_records(s, 0, s, True)
            with dve.Fori(1, EG // 2) as i:
                for s in range(2):
                    make_records(2 * i + s, i, s, False)
            dve.wait_ge(rec_made, 3 * EG + 6)

            for q in (onehot_made, src_onehot_made, src_out, z_ready, msg_ready):
                dve.sem_inc(q, 2)
            dve.sem_inc(rec_used, RECS)

            dve.wait_ge(src_cols_in, 16)
            dve.tensor_copy(src_cols16[:], src_cols[:]).then_inc(src_cols_cast, 1)

            def split(nodes):
                step(dve.tensor_copy(src_split[:, :, 0, :], nodes))
                step(dve.tensor_tensor(v, nodes, src_split[:, :, 0, :], ALU.subtract))
                step(dve.tensor_copy(src_split[:, :, 1, :], v))
                step(dve.tensor_tensor(v, v, src_split[:, :, 1, :], ALU.subtract))
                dve.tensor_copy(src_split[:, :, 2, :], v).then_inc(split_ready, 1)

            def norm(t, res):
                step(dve.tensor_reduce(stat[:, 0, :], v, X_AXIS, ALU.add))
                step(dve.tensor_scalar(stat[:, 0, :], stat[:, 0, :], 1.0 / HID, None, ALU.mult))
                step(dve.tensor_tensor(v, v, stat[:, 0, :].unsqueeze(2).to_broadcast([P, NB, HID]), ALU.subtract))
                step(dve.tensor_tensor(res[:], v, v, ALU.mult))
                dve.tensor_reduce(stat[:, 1, :], res[:], X_AXIS, ALU.add).then_inc(var_ready, 1)
                dve.wait_ge(sd_ready, t)
                step(dve.reciprocal(stat[:, 3, :], stat[:, 2, :]))
                dve.tensor_tensor(res[:], v, stat[:, 3, :].unsqueeze(2).to_broadcast([P, NB, HID]),
                                  ALU.mult).then_inc(normed, 1)

            for l in range(2 * LAYERS):
                if 0 < l < LAYERS:
                    destination_terms(l)
                if l >= LAYERS:
                    k = l - LAYERS
                    if k == 0:
                        for c in range(-(-NB // 8)):
                            n = min(8, NB - 8 * c)
                            dve.wait_ge(back_mm, c + 1)
                            dve.tensor_tensor(v[:, 8 * c:8 * c + n, :],
                                              work[c % 2][:, 0:n * HID].rearrange("p (b f) -> p b f", b=n),
                                              xn[:, 8 * c:8 * c + n, :], ALU.add).then_inc(back_out, 1)
                        dve.wait_ge(back_out, -(-NB // 8))
                        norm(1, x1)
                        dve.wait_ge(rel_in, 16 * 3 * LAYERS)
                    for b in range(NB):
                        dve.wait_ge(y_out, NB * k + b + 1)
                        dve.tensor_tensor(root[:, b, :], work[b % 4][:, R * HID:(R + 1) * HID], b_rel[k][:],
                                          ALU.add).then_inc(root_out, 1)

                dve.wait_ge(src_terms_out, CH * min(l + 1, LAYERS))
                split(hn[:] if l != LAYERS else x1[:])

                def one_hots(i, u, l=l):
                    n = l * NG + 4 * i + u
                    s = u % 2
                    rec = rec_in[u]
                    dve.wait_ge(rec_loaded[u], 32 * (l * USES[u] + i + 1))
                    if l <= LAYERS:
                        dve.wait_ge(onehot_turned, reusable(n))
                    dve.wait_ge(onehot_out, reusable(n))
                    for j in range(GT):
                        ins = dve.tensor_scalar(onehot_b[s][:, j, :], iota_b[:], rec[:, j, PLACE:PLACE + 1], None,
                                                ALU.is_equal)
                    ins.then_inc(onehot_made, 1)
                    dve.wait_ge(src_gathered, reusable(n))
                    dve.tensor_tensor(src_onehot[s], src_in[u][:].unsqueeze(1).to_broadcast([P, NB, P]),
                                      node_grid[:],
                                      ALU.is_equal).then_inc(src_onehot_made, 1)

                def source_sum(i, u, l=l):
                    n = l * NG + 4 * i + u
                    s = u % 2
                    dve.wait_ge(src_gathered, done(n))
                    if l >= LAYERS:
                        dve.wait_ge(terms_gathered, reusable(n))
                    dve.tensor_reduce(src_row[s][:, 0:HID], src_ps[:, 0:3 * HID].rearrange("p (k f) -> p f k", k=3),
                                      X_AXIS, ALU.add).then_inc(src_out, 1)

                def messages(i, u, nt, l=l):
                    n = l * NG + 4 * i + u
                    s = u % 2
                    rec = rec_in[u]
                    types = rec[:, :, TYPE:TYPE + 1].to_broadcast([P, GT, R])
                    type_row = iota_r[:].unsqueeze(1).to_broadcast([P, GT, R])
                    dve.wait_ge(summed, reusable(n))
                    if l < LAYERS:
                        dve.tensor_tensor(msg[s][:, :, HID:REC], type_row, types, ALU.is_equal)
                        source_sum(i, u)
                        dve.wait_ge(rows_in[s], rows_landed(l, i, u, nt))
                        dve.wait_ge(msg_ready, reusable(n))
                        dve.tensor_tensor(z[s][:, 0:GP, :], rows[s][:], rec[:, 0:GP, 0:HID], ALU.add)
                        dve.wait_ge(src_out, done(n))
                        dve.tensor_tensor(z[s][:, GP, :], src_row[s][:, 0:HID], rec[:, GP, 0:HID],
                                          ALU.add).then_inc(rec_used, 1)
                        dve.wait_ge(terms_gathered, done(n))
                        dve.wait_ge(rec_used, done(n, RECS))
                        dve.tensor_tensor(z[s][:], z[s][:], gathered_ps[s][:].rearrange("p (j f) -> p j f", j=GT),
                                          ALU.add).then_inc(z_ready, 1)
                    else:
                        k = l - LAYERS
                        m = 4 * (n - LAYERS * NG)
                        slots = weight[:, bass.ds(GT * (n - l * NG), GT), :]
                        last = weight[:, bass.ds(GT * (n - l * NG) + GP, 1), :].rearrange("p a r -> p (a r)")
                        if k == 0:
                            dve.tensor_tensor(is_type[s][:], type_row, types, ALU.is_equal).then_inc(share_step, 1)
                            dve.wait_ge(share_step, m + 1)
                            dve.wait_ge(terms_gathered, done(n))
                            dve.tensor_tensor(slots, is_type[s][:],
                                              gathered_ps[s][:, 0:GT * R].rearrange("p (j r) -> p j r", j=GT),
                                              ALU.mult).then_inc(share_step, 1)
                        else:
                            dve.wait_ge(terms_gathered, done(n))
                            dve.sem_inc(share_step, 2)
                        dve.wait_ge(share_step, m + 2)
                        dve.tensor_tensor(by_type[s][:],
                                          gathered_ps[s][:, R * HID:2 * R * HID].rearrange("p (r f) -> p r f", r=R),
                                          last.unsqueeze(2).to_broadcast([P, R, HID]),
                                          ALU.mult).then_inc(z_ready, 1)
                        dve.tensor_reduce(share[s][:], slots, X_AXIS, ALU.add).then_inc(share_step, 1)
                        dve.wait_ge(z_ready, done(n))
                        dve.tensor_reduce(msg[s][:, GP, 0:HID], by_type[s][:].rearrange("p r f -> p f r"),
                                          X_AXIS, ALU.add).then_inc(share_step, 1)
                        dve.wait_ge(share_step, m + 3)
                        dve.wait_ge(rows_in[s], rows_landed(l, i, u, nt))
                        dve.tensor_tensor(msg[s][:, 0:GP, 0:HID], rows[s][:],
                                          share[s][:, 0:GP].unsqueeze(2).to_broadcast([P, GP, HID]),
                                          ALU.mult).then_inc(msg_ready, 1)
                        dve.wait_ge(msg_ready, done(n))
                        dve.sem_inc(rec_used, 1)

                staged_groups(dve, one_hots, messages, before=source_sum if l >= LAYERS else None)
                dve.wait_ge(summed, done(l * NG + NG - 1))

                if l < LAYERS:
                    for c in range(BANKS):
                        bs = bank_blocks(c)
                        ins = dve.tensor_reduce(deg[:, 0, bs[0]:bs[-1] + 1], bank_view(sums_v, c, HID, REC),
                                                X_AXIS, ALU.add)
                    step(ins)
                    dve.tensor_scalar(mean_n[:, :, HID], deg[:, 0, :], 1.0, None, ALU.min)
                    step(dve.tensor_scalar(deg[:, 1, :], deg[:, 0, :], 1.0, None, ALU.max))
                    step(dve.reciprocal(deg[:, 2, :], deg[:, 1, :]))
                    for c in range(BANKS):
                        bs = bank_blocks(c)
                        ins = dve.tensor_tensor(mean_n[:, bs[0]:bs[-1] + 1, 0:HID], bank_view(sums_v, c, 0, HID),
                                                deg[:, 2, bs[0]:bs[-1] + 1].unsqueeze(2)
                                                .to_broadcast([P, len(bs), HID]), ALU.mult)
                        if l == LAYERS - 1:
                            ins = dve.tensor_scalar(bank_view(dst_terms, c, HID, REC), bank_view(sums_v, c, HID, REC),
                                                    1.0, None, ALU.max)
                    if l == LAYERS - 1:
                        step(ins)
                        for c in range(BANKS):
                            ins = dve.reciprocal(bank_view(dst_terms, c, HID, REC), bank_view(dst_terms, c, HID, REC))
                    ins.then_inc(mean_ready, 1)
                    for c in range(CH):
                        w = P * len(chunk(c))
                        dve.wait_ge(delta_mm, CH * l + c + 1)
                        at = cat[0:HID, 512 * c:512 * c + w]
                        dve.scalar_tensor_tensor(out=at, in0=work[2 + c % 2][0:HID, 0:w], scalar=b2n_c[:, 0:1],
                                                 in1=at, op0=ALU.add, op1=ALU.add).then_inc(state_ready, 1)
                else:
                    to = v if k == LAYERS - 1 else hn[:]
                    for c in range(BANKS):
                        bs = bank_blocks(c)
                        ins = dve.tensor_tensor(to[:, bs[0]:bs[-1] + 1, :], bank_view(sums_v, c, 0, HID),
                                                root[:, bs[0]:bs[-1] + 1, :], ALU.add)
                    step(ins)
                    if k < LAYERS - 1:
                        dve.tensor_scalar(hn[:], hn[:], 0.0, None, ALU.max).then_inc(layer_out, 1)
                    else:
                        step(dve.tensor_tensor(v, v, x1[:], ALU.add))
                        norm(2, hn)


RANKED = 11


_L0 = ['L0_gnn_' + n for n in ('W1e', 'b1e', 'W2e', 'b2e', 'W1n', 'b1n', 'W2n', 'b2n')]
_INS = ['x', 'src', 'dst', 'edge_attr_16', 'edge_type_4'] + _L0 + [
    f'L1_gnn_{n}{l}' for n in ('W', 'root', 'b') for l in range(3)]


def kernel(**inputs):
    import numpy as _np
    import concourse.bacc as _bacc
    from concourse import mybir as _mybir
    from concourse.bass_utils import run_bass_kernel_spmd as _run

    nc = _bacc.Bacc("TRN2", target_bir_lowering=False, num_devices=1)
    arrays, args = {}, []
    for name in _INS:
        a = _np.ascontiguousarray(inputs[name])
        arrays[f"in_{name}_dram"] = a
        args.append(nc.dram_tensor(f"in_{name}_dram", a.shape, _mybir.dt.from_np(a.dtype), kind="ExternalInput").ap())
    out = nc.dram_tensor("out_0_dram", args[0].shape, _mybir.dt.float32, kind="ExternalOutput").ap()
    gnn_kernel(nc, *args[:13], args[13:16], args[16:19], args[19:22], out)
    r = _run(nc, [arrays], core_ids=[0])
    return r.results[0]["out_0_dram"]
```

```python
from contextlib import ExitStack

import concourse.bass as bass
from concourse import mybir

ALU = mybir.AluOpType
ACT = mybir.ActivationFunctionType
X_AXIS = mybir.AxisListType.X
F32 = mybir.dt.float32
BF16 = mybir.dt.bfloat16
I32 = mybir.dt.int32
U32 = mybir.dt.uint32
I16 = mybir.dt.int16
U16 = mybir.dt.uint16

P = 128
HID = 64
EPS = 1e-5

GT = 8
REC = HID + 4
ROW0, ROW1, PLACE, TYPE = HID, HID + 1, HID + 2, HID + 3
PER_BANK = 512 // REC


def gnn_kernel(nc, x, src, dst, edge_attr, edge_type, W1e, b1e, W2e, b2e, W1n, b1n, W2n, b2n,
               rel_w, rel_root, rel_b, out):
    N = x.shape[0]
    E, ED = edge_attr.shape
    R = rel_w[0].shape[0]
    NB = -(-N // P)
    NP = NB * P
    LAST = N - (NB - 1) * P
    EP = 125
    EC = E // EP
    EG = EC // GT
    TILES = (E + NB * (P - 1)) // P
    NG = -(-TILES // GT)
    EARLY = 16
    RANKED_PER_PAIR = 4
    QUADS = NG // 4
    GP = GT - 1
    LAST_TILES = TILES - (NG - 1) * GT
    BANKS = -(-NB // PER_BANK)
    CH = -(-NB // 4)
    ROOTS = -(-NB // 8)
    LAYERS = 3
    assert EP * EC == E and EG % 2 == 0 and RANKED_PER_PAIR * EARLY // 2 >= NB and NG % 4 == 1 and GT * ED == P and R == 4

    recs = nc.dram_tensor("recs", [NG * GT * P, REC], F32, kind="Internal").ap()
    table0 = nc.dram_tensor("table0", [NP, HID], F32, kind="Internal").ap()
    table1 = nc.dram_tensor("table1", [NP * R, HID], F32, kind="Internal").ap()
    src_rows = nc.dram_tensor("src_rows", [NG, 2, P], I16, kind="Internal").ap()
    recs_by_group = recs.rearrange("(g p j) w -> p g (j w)", p=P, j=GT)
    tile_src = recs.rearrange("(g p j) w -> g p j w", p=P, j=GT)[:, :, :, ROW0:ROW0 + 1]

    def chunk(c):
        return range(4 * c, min(4 * c + 4, NB))

    with ExitStack() as ctx:
        def sb(name, shape, dt=F32):
            return ctx.enter_context(nc.sbuf_tensor(name, shape, dt))

        def ps(name, shape, dt=F32):
            return ctx.enter_context(nc.psum_tensor(name, shape, dt))

        def sem(name):
            return ctx.enter_context(nc.semaphore(name))

        ident = sb("ident", [P, P])
        ident_b = sb("ident_b", [P, P], BF16)
        ones = sb("ones", [P, P])
        before = sb("before", [P, P])
        iota_i = sb("iota_i", [P, P], I32)
        iota_b = sb("iota_b", [P, P], BF16)
        iota_r = sb("iota_r", [P, R])
        tile_i = sb("tile_i", [P, GT], I32)
        node_i = sb("node_i", [P, NB], I32)
        node_grid = sb("node_grid", [P, NB, P], I16)
        tile_f = sb("tile_f", [P, GT])
        block_step = sb("block_step", [P, NB - 1])
        zeros_b = sb("zeros_b", [P, 512], BF16)
        ones_e = sb("ones_e", [P, EC], BF16)
        eps = sb("eps", [P, 1])
        we8 = sb("we8", [P, GT, HID])
        w_ab = sb("w_ab", [HID, 2 * HID])
        b1e_all = sb("b1e_all", [P, HID])
        w2e = sb("w2e", [HID + 1, P])
        w1n = sb("w1n", [P, HID])
        w2n = sb("w2n", [HID, HID])
        b1n_c = sb("b1n_c", [HID, 1])
        b2n_c = sb("b2n_c", [HID, 1])
        w_rel = [sb(f"w_rel{l}", [HID, R + 1, HID]) for l in range(LAYERS)]
        b_rel = [sb(f"b_rel{l}", [P, HID]) for l in range(LAYERS)]
        xn = sb("xn", [P, NB, HID])
        x1 = sb("x1", [P, NB, HID])
        hn = sb("hn", [P, NB, HID])
        cat = sb("cat", [P, NP])
        dst_terms = sb("dst_terms", [P, BANKS, 512])
        terms_flat = dst_terms[:].rearrange("p a b -> p (a b)")
        deg = sb("deg", [P, 4, NB])
        stat = sb("stat", [P, 4, NB])
        arena1 = sb("arena1", [P, 10240])
        arena2 = sb("arena2", [P, 8 * EC + 1664])
        in_block = arena1[0:EP, 0:NB * EC // 2].bitcast(BF16).rearrange("p (k e) -> p k e", k=NB)
        y_rows = arena1[:, 0:NB * R * HID].rearrange("p (b w) -> p b w", b=NB)
        root = arena1[:, NB * R * HID:NB * (R + 1) * HID].rearrange("p (b w) -> p b w", b=NB)
        v = arena1[:, NB * (R + 1) * HID:NB * (R + 2) * HID].rearrange("p (b w) -> p b w", b=NB)

        weight = arena2[:, 0:NG * GT * R].rearrange("p (t r) -> p t r", r=R)

        def edge_row(k, dt=F32):
            return arena2[0:EP, k * EC:(k + 1) * EC].bitcast(dt)

        src_i, dst_i, type_i, part_i = (edge_row(k, I32) for k in range(4))
        block_f, rank, slot_f = (edge_row(k) for k in range(4, 7))
        slot_i = edge_row(7, I32)
        w_pair = arena2[:, NG * GT * R:NG * GT * R + (LAYERS - 1) * 2 * R * HID].rearrange(
            "p (l m w) -> p l m w", l=LAYERS - 1, m=2)
        mean_t = arena2[0:HID + 1, 0:NP]
        hidden = arena2[0:HID, NP:2 * NP]
        mean_n = arena2[:, 2 * NP:2 * NP + NB * (HID + 1)].rearrange("p (b w) -> p b w", b=NB)
        arena3 = sb("arena3", [P, 4 * EC])
        meta = arena3[0:EP, :].rearrange("p (e w) -> p e w", w=4)
        meta_i = meta.bitcast(I32)
        src_onehot = [arena3[:, s * NB * P // 2:(s + 1) * NB * P // 2].bitcast(BF16)
                      .rearrange("p (b e) -> p b e", b=NB) for s in range(2)]
        arena4 = sb("arena4", [P, NB * 3 * HID // 2])
        addr = arena4[0:EP, 0:EC].bitcast(I32)
        src_split = arena4[:].bitcast(BF16).rearrange("p (b k f) -> p b k f", b=NB, k=3)
        count = sb("count", [EP, NB])
        tiles_i = sb("tiles_i", [P, NB], I32)
        tiles_f = sb("tiles_f", [P, NB])
        tiles_end = sb("tiles_end", [P, NB])
        first_slot = sb("first_slot", [P, NB])
        passed = sb("passed", [P, GT, NB - 1])
        off_f = sb("off_f", [P, GT])
        off_i = sb("off_i", [P, GT], I32)
        offsets = sb("offsets", [1, NG * GT], I32)
        ea = [sb(f"ea{s}", [EP, P]) for s in range(2)]
        ea_t = [sb(f"ea_t{s}", [P, EP]) for s in range(2)]
        addr_out = [sb(f"addr_out{s}", [EP, GT], I32) for s in range(2)]
        rec_in = [sb(f"rec_in{s}", [P, GT, REC]) for s in range(4)]
        src_in = [sb(f"src_in{s}", [P, 1 + s % 2, P], I16) for s in range(4)]
        rows = [sb(f"rows{s}", [P, GP, HID]) for s in range(2)]
        src_row = [sb(f"src_row{s}", [P, 2 * HID]) for s in range(2)]
        src_t = [sb(f"src_t{s}", [P, P]) for s in range(2)]
        by_type = [sb(f"by_type{s}", [P, 1 + s, R, HID]) for s in range(2)]
        onehot_b = [sb(f"onehot_b{s}", [P, GT, P], BF16) for s in range(2)]
        onehot = [sb(f"onehot{s}", [P, GT, P]) for s in range(2)]
        onehot_ts = sb("onehot_ts", [P, 2, GT, P])
        onehot_t = [onehot_ts[:, s, :, :] for s in range(2)]
        src_onehot_late = (onehot_ts[:].rearrange("p s j n -> p (s j n)")[:, 0:NB * P // 2].bitcast(BF16)
                           .rearrange("p (b e) -> p b e", b=NB))
        src_onehot_early = arena1[:, 0:NB * P // 2].bitcast(BF16).rearrange("p (b e) -> p b e", b=NB)

        def source_one_hot(l, s, m):
            if m == 0:
                return src_onehot[s]
            return src_onehot_early if l < LAYERS else src_onehot_late

        z = [sb(f"z{s}", [P, GT, HID]) for s in range(2)]
        src_cols = z[0][0:NG, 0:2 * P // HID, :].rearrange("g j f -> g (j f)").rearrange("g (m p) -> g m p", m=2)
        src_cols16 = (z[1][0:NG, 0:P // HID, :].rearrange("g j f -> g (j f)").bitcast(I16)
                      .rearrange("g (m p) -> g m p", m=2))
        msg = [sb(f"msg{s}", [P, GT, REC]) for s in range(2)]
        rec_out = [msg[s][0:EP, :, :] for s in range(2)]
        no_edge = rec_in[3]
        is_type = [sb(f"is_type{s}", [P, GT, R]) for s in range(2)]
        share = [sb(f"share{s}", [P, GT]) for s in range(2)]

        sums = ps("sums", [P, BANKS * 512])
        sums_v = sums[:].rearrange("p (a b) -> p a b", a=BANKS)
        work = [ps(f"work{k}", [P, 512]) for k in range(4)]
        turned = work[0][:].bitcast(BF16)
        gathered_ps = [work[2 + s] for s in range(2)]

        def src_ps(l, s):
            return work[s if l > LAYERS else 1]

        def bank_blocks(c):
            return range(PER_BANK * c, min(PER_BANK * c + PER_BANK, NB))

        def bank_view(t, c, a, b):
            n = len(bank_blocks(c))
            return t[:, c, 0:n * REC].rearrange("p (i w) -> p i w", w=REC)[:, :, a:b]

        pool_step = sem("pool_step")
        consts_made = sem("consts_made")
        consts_cast = sem("consts_cast")
        weights_in = sem("weights_in")
        zeroed = sem("zeroed")
        rel_in = sem("rel_in")
        pair_zeroed = sem("pair_zeroed")
        pair_in = sem("pair_in")
        x_in = sem("x_in")
        edges_in = sem("edges_in")
        recs_blank = sem("recs_blank")
        dve_step = sem("dve_step")
        turn_mm = sem("turn_mm")
        turn_out = sem("turn_out")
        term_mm = sem("term_mm")
        src_terms_out = sem("src_terms_out")
        dst_terms_out = sem("dst_terms_out")
        table_stored = sem("table_stored")
        mean_ready = sem("mean_ready")
        mean_turned = sem("mean_turned")
        mean_t_out = sem("mean_t_out")
        agg_mm = sem("agg_mm")
        agg_out = sem("agg_out")
        hidden_mm = sem("hidden_mm")
        hidden_out = sem("hidden_out")
        delta_mm = sem("delta_mm")
        state_ready = sem("state_ready")
        back_mm = sem("back_mm")
        back_out = sem("back_out")
        var_ready = sem("var_ready")
        sd_ready = sem("sd_ready")
        normed = sem("normed")
        rel_mm = sem("rel_mm")
        y_out = sem("y_out")
        root_mm = sem("root_mm")
        root_out = sem("root_out")
        layer_out = sem("layer_out")
        stored = sem("stored")
        counted = sem("counted")
        count_mm = sem("count_mm")
        off_ready = sem("off_ready")
        offsets_in = sem("offsets_in")
        ea_in = [sem(f"ea_in{s}") for s in range(2)]
        ea_turned = sem("ea_turned")
        ea_t_out = sem("ea_t_out")
        term_e_mm = sem("term_e_mm")
        rec_made = sem("rec_made")
        scatter_go = sem("scatter_go")
        rec_stored = [sem(f"rec_stored{s}") for s in range(2)]
        rec_loaded = [sem(f"rec_loaded{s}") for s in range(4)]
        src_loaded = [sem(f"src_loaded{s}") for s in range(4)]
        rec_used = sem("rec_used")
        split_step = sem("split_step")
        split_ready = sem("split_ready")
        src_cols_in = sem("src_cols_in")
        src_rows_stored = sem("src_rows_stored")
        src_onehot_made = sem("src_onehot_made")
        src_gathered = sem("src_gathered")
        src_out = sem("src_out")
        src_cols_cast = sem("src_cols_cast")
        src_turned = sem("src_turned")
        src_t_out = sem("src_t_out")
        gather_go = sem("gather_go")
        rows_in = [sem(f"rows_in{s}") for s in range(2)]
        onehot_made = sem("onehot_made")
        onehot_turned = sem("onehot_turned")
        onehot_out = sem("onehot_out")
        onehot_t_out = sem("onehot_t_out")
        terms_gathered = sem("terms_gathered")
        z_ready = sem("z_ready")
        msg_ready = sem("msg_ready")
        summed = sem("summed")
        share_step = sem("share_step")

        def done(n, start=2):
            return n + 1 + start

        def reusable(n):
            return n + 1

        RECS = 4
        USES = [QUADS + 1, QUADS, QUADS, QUADS]

        def by_dma(l, u):
            return GP - 1 if (l < LAYERS and u == 3) or (l > LAYERS and u % 2) else GP

        def rows_of_four(l, s):
            return 16 * (by_dma(l, s) + by_dma(l, s + 2))

        def rows_of_layer(l, s):
            return rows_of_four(l, s) * QUADS + (16 * LAST_TILES if s == 0 else 0)

        def rows_landed(l, i, u, nt):
            before = sum(rows_of_layer(k, u % 2) for k in range(l)) + (16 * by_dma(l, u - 2) if u >= 2 else 0)
            return before + rows_of_four(l, u % 2) * i + 16 * min(nt, by_dma(l, u))

        def groups(eng, body):
            with eng.Fori(0, QUADS) as i:
                for u in range(4):
                    body(i, u, GP)
            body(QUADS, 0, LAST_TILES)

        def staged_groups(eng, ahead, body, body_first=False, before=None):
            ahead(0, 0)
            with eng.Fori(0, QUADS) as i:
                for u in range(4):
                    if before:
                        before(i, u)
                    if body_first:
                        body(i, u, GP)
                    ahead(i + (u + 1) // 4, (u + 1) % 4)
                    if not body_first:
                        body(i, u, GP)
            if before:
                before(QUADS, 0)
            body(QUADS, 0, LAST_TILES)

        block = ctx.enter_context(nc.Block())

        @block.sync
        def _(sp):
            for t, a in ((dst_i, dst), (src_i, src), (type_i, edge_type)):
                sp.dma_start(t, a.rearrange("(p e) -> p e", p=EP)).then_inc(edges_in, 16)
            sp.wait_ge(zeroed, 1)
            sp.dma_start(xn[:, 0:NB - 1, :],
                         x[0:(NB - 1) * P, :].rearrange("(b p) f -> p b f", p=P)).then_inc(x_in, 16)
            sp.dma_start(xn[0:LAST, NB - 1, :], x[(NB - 1) * P:N, :]).then_inc(x_in, 16)

            attr = edge_attr.rearrange("(p e) f -> p (e f)", p=EP)

            def load_attr(g, s):
                sp.wait_ge(ea_turned, g + 1)
                sp.dma_start(ea[s][:], attr[:, bass.ds(g * P, P)]).then_inc(ea_in[s], 16)

            def store_table0(l):
                for c in range(CH):
                    b, e = chunk(c)[0], chunk(c)[-1] + 1
                    sp.wait_ge(src_terms_out, CH * l + c + 1)
                    sp.dma_start(table0[b * P:e * P, :].rearrange("(b p) f -> p b f", p=P),
                                 hn[:, b:e, :]).then_inc(table_stored, 16)

            store_table0(0)
            sp.wait_ge(off_ready, 1)
            sp.dma_start(offsets[0:1, :], off_i[0:NG, :]).then_inc(offsets_in, 16)
            with sp.Fori(0, EG // 2) as i:
                for s in range(2):
                    load_attr(2 * i + s, s)
            for s in range(2):
                sp.wait_ge(rec_stored[s], 16 * GT * (EG // 2))

            def load_records(l, i, u):
                g = 4 * i + u
                sp.wait_ge(rec_used, done(l * NG + g - 4, RECS))
                sp.dma_start(rec_in[u][:].rearrange("p j w -> p (j w)"),
                             recs_by_group[:, bass.ds(g, 1), :].rearrange("p a w -> p (a w)")
                             ).then_inc(rec_loaded[u], 16)

            def load_sources(l, i, u):
                m = GT - by_dma(l, u)
                sp.dma_start(src_in[u][:, 0:m, :], src_rows[bass.ds(4 * i + u, 1), 0:m, :].to_broadcast([P, m, P])
                             ).then_inc(src_loaded[u], 16)

            for u in range(4):
                load_records(0, 0, u)
            for m in range(2):
                sp.dma_start(src_cols[:, m, :].unsqueeze(2), tile_src[:, :, GT - 1 - m, :],
                             allow_slow_non_contiguous=True).then_inc(src_cols_in, 16)
            sp.wait_ge(src_cols_cast, 1)
            sp.dma_start(src_rows, src_cols16).then_inc(src_rows_stored, 16)
            sp.wait_ge(src_rows_stored, 16)
            for u in range(4):
                load_sources(0, 0, u)

            for l in range(2 * LAYERS):
                if 0 < l < LAYERS:
                    store_table0(l)
                if l >= LAYERS:
                    k = l - LAYERS
                    for c in range(CH):
                        b, e = chunk(c)[0], chunk(c)[-1] + 1
                        sp.wait_ge(y_out, NB * k + e)
                        sp.dma_start(table1[b * P * R:e * P * R, :].rearrange("(b p r) f -> p b (r f)", p=P, r=R),
                                     y_rows[:, b:e, :]).then_inc(table_stored, 16)
                with sp.Fori(1 if l == 0 else 0, QUADS) as i:
                    for u in range(4):
                        load_records(l, i, u)
                        load_sources(l, i, u)
                load_records(l, QUADS, 0)
                load_sources(l, QUADS, 0)
                if l == LAYERS:
                    sp.wait_ge(pair_zeroed, 1)
                    for k in range(1, LAYERS):
                        for m in range(2):
                            sp.dma_start(w_pair[m * HID:(m + 1) * HID, k - 1, 1 - m, :]
                                         .rearrange("i (r o) -> i r o", r=R),
                                         rel_w[k].rearrange("r i o -> i r o")).then_inc(pair_in, 16)
            sp.wait_ge(normed, 2)
            sp.dma_start(out[0:(NB - 1) * P, :].rearrange("(b p) f -> p b f", p=P),
                         hn[:, 0:NB - 1, :]).then_inc(stored, 16)
            sp.dma_start(out[(NB - 1) * P:N, :], hn[0:LAST, NB - 1, :]).then_inc(stored, 16)
            sp.wait_ge(stored, 32)

        @block.gpsimd
        def _(pool):
            pool.memset(ident[:], 0.0).then_inc(pool_step, 1)
            pool.memset(ones[:], 1.0).then_inc(pool_step, 1)
            pool.iota(iota_i[:], [[1, P]], base=0, channel_multiplier=0).then_inc(consts_made, 1)
            pool.iota(tile_i[:], [[1, GT]], base=0, channel_multiplier=GT).then_inc(consts_made, 1)
            pool.iota(node_i[:], [[P, NB]], base=0, channel_multiplier=1).then_inc(consts_made, 1)
            pool.wait_ge(pool_step, 2)
            pool.affine_select(out=ident[:], in_=ident[:], compare_op=ALU.not_equal, fill=1.0,
                               base=0, pattern=[[-1, P]], channel_multiplier=1).then_inc(consts_made, 1)
            pool.affine_select(out=before[:], in_=ones[:], compare_op=ALU.is_gt, fill=0.0,
                               base=0, pattern=[[1, P]], channel_multiplier=-1).then_inc(consts_made, 1)

            pool.wait_ge(recs_blank, 16)
            with pool.Fori(0, EG // 2) as i:
                for s in range(2):
                    pool.wait_ge(rec_made, 3 * (2 * i + s) + 9)
                    pool.sem_inc(scatter_go, 1)
                    for j in range(GT):
                        pool.indirect_dma_start(
                            recs, bass.IndirectOffsetOnAxis(ap=addr_out[s][:, j:j + 1].bitcast(U32), axis=0),
                            rec_out[s][:, j, :], None).then_inc(rec_stored[s], 16)

            for l in range(2 * LAYERS):
                pool.wait_ge(table_stored, 16 * CH * (l + 1))
                table = table0 if l < LAYERS else table1
                field = ROW0 if l < LAYERS else ROW1

                def gather(i, u, nt, l=l):
                    n = l * NG + 4 * i + u
                    s = u % 2
                    pool.wait_ge(rec_used, done(n - 2, RECS))
                    pool.wait_ge(rec_loaded[u], 16 * (l * USES[u] + i + 1))
                    pool.sem_inc(gather_go, 1)
                    for j in range(min(nt, by_dma(l, u))):
                        pool.indirect_dma_start(
                            rows[s][:, j, :], None, table,
                            bass.IndirectOffsetOnAxis(ap=rec_in[u][:, j, field:field + 1].bitcast(U32), axis=0)
                        ).then_inc(rows_in[s], 16)

                groups(pool, gather)

        @block.scalar
        def _(act):
            act.wait_ge(zeroed, 1)
            for i in range(GT):
                act.dma_start(we8[ED * i:ED * (i + 1), i, :], W1e[2 * HID:2 * HID + ED, :]).then_inc(weights_in, 16)
            act.dma_start(w_ab[:, 0:HID], W1e[0:HID, :]).then_inc(weights_in, 16)
            act.dma_start(w_ab[:, HID:2 * HID], W1e[HID:2 * HID, :]).then_inc(weights_in, 16)
            act.dma_start(b1e_all[:], b1e.partition_broadcast(P)).then_inc(weights_in, 16)
            act.dma_start(w2e[0:HID, HID:P], W2e).then_inc(weights_in, 16)
            act.dma_start(w2e[HID:HID + 1, HID:P], b2e.rearrange("(a f) -> a f", a=1)).then_inc(weights_in, 16)
            act.dma_start(w1n[:], W1n).then_inc(weights_in, 16)
            act.dma_start(w2n[:], W2n).then_inc(weights_in, 16)
            act.dma_start(b1n_c[:], b1n.rearrange("(f a) -> f a", a=1)).then_inc(weights_in, 16)
            act.dma_start(b2n_c[:], b2n.rearrange("(f a) -> f a", a=1)).then_inc(weights_in, 16)
            act.dma_start(recs_by_group, no_edge[:].rearrange("p j w -> p (j w)").unsqueeze(1)
                          .to_broadcast([P, NG, GT * REC])).then_inc(recs_blank, 16)
            for l in range(LAYERS):
                act.dma_start(w_rel[l][:, 0:R, :], rel_w[l].rearrange("r i o -> i r o")).then_inc(rel_in, 16)
                act.dma_start(w_rel[l][:, R, :], rel_root[l]).then_inc(rel_in, 16)
                act.dma_start(b_rel[l][:], rel_b[l].partition_broadcast(P)).then_inc(rel_in, 16)

            def turn_state(t):
                for c in range(CH):
                    w = P * len(chunk(c))
                    act.wait_ge(turn_mm, CH * t + c + 1)
                    act.copy(cat[0:HID, 512 * c:512 * c + w], work[c % 2][0:HID, 0:w]).then_inc(turn_out, 1)

            def source_terms(l):
                for c in range(CH):
                    n = len(chunk(c))
                    act.wait_ge(term_mm, CH * l + c + 1)
                    act.copy(hn[:, 4 * c:4 * c + n, :],
                             work[c % 4][:, 0:P * n].rearrange("p (b w) -> p b w", b=n)[:, :, 0:HID]
                             ).then_inc(src_terms_out, 1)

            turn_state(0)
            source_terms(0)

            for q in (ea_t_out, onehot_out, onehot_t_out):
                act.sem_inc(q, 2)
            with act.Fori(0, EG // 2) as i:
                for s in range(2):
                    g = 2 * i + s
                    act.wait_ge(ea_turned, done(g))
                    act.wait_ge(term_e_mm, reusable(g))
                    act.copy(ea_t[s][:], work[s][:, 0:EP]).then_inc(ea_t_out, 1)

            for l in range(2 * LAYERS):
                if 0 < l < LAYERS:
                    source_terms(l)
                if l >= LAYERS:
                    k = l - LAYERS
                    if k == 0:
                        act.wait_ge(var_ready, 1)
                        act.activation(stat[:, 2, :], stat[:, 1, :], ACT.Sqrt, bias=eps[:, 0:1],
                                       scale=1.0 / HID).then_inc(sd_ready, 1)
                    turn_state(1 + k)
                    for b in range(NB):
                        act.wait_ge(rel_mm, NB * k + b + 1)
                        act.copy(y_rows[:, b, :], work[b % 4][:, 0:R * HID]).then_inc(y_out, 1)

                def one_hots(i, u, l=l):
                    n = l * NG + 4 * i + u
                    s = u % 2
                    if l <= LAYERS:
                        act.wait_ge(onehot_turned, done(n))
                        act.wait_ge(terms_gathered, reusable(n))
                        act.copy(onehot_t[s].rearrange("p j n -> p (j n)"), turned).then_inc(onehot_t_out, 1)
                    act.wait_ge(onehot_made, done(n))
                    act.wait_ge(summed, reusable(n))
                    act.copy(onehot[s][:], onehot_b[s][:]).then_inc(onehot_out, 1)

                def messages(i, u, nt, l=l):
                    n = l * NG + 4 * i + u
                    s = u % 2
                    if l >= LAYERS:
                        m = n - LAYERS * NG
                        act.wait_ge(src_turned, m + 1)
                        act.wait_ge(terms_gathered, reusable(n))
                        h = HID * (GT - by_dma(l, u))
                        act.copy(src_t[s][0:h, :], gathered_ps[s][0:h, HID:HID + P]).then_inc(src_t_out, 1)
                    if l < LAYERS:
                        act.wait_ge(z_ready, done(n))
                        act.activation(msg[s][:, :, 0:HID], z[s][:], ACT.Silu).then_inc(msg_ready, 1)

                staged_groups(act, one_hots, messages, body_first=l >= LAYERS)

                if l < LAYERS:
                    for c in range(CH):
                        w = P * len(chunk(c))
                        act.wait_ge(mean_turned, CH * l + c + 1)
                        act.copy(mean_t[:, 512 * c:512 * c + w], work[c % 2][0:HID + 1, 0:w]).then_inc(mean_t_out, 1)
                    for c in range(CH):
                        w = P * len(chunk(c))
                        act.wait_ge(agg_mm, CH * l + c + 1)
                        act.copy(cat[HID:P, 512 * c:512 * c + w], work[2 + c % 2][HID:P, 0:w]).then_inc(agg_out, 1)
                    for c in range(CH):
                        w = P * len(chunk(c))
                        act.wait_ge(hidden_mm, CH * l + c + 1)
                        act.activation(hidden[:, 512 * c:512 * c + w], work[c % 2][0:HID, 0:w], ACT.Silu,
                                       bias=b1n_c[:, 0:1]).then_inc(hidden_out, 1)
            act.wait_ge(var_ready, 2)
            act.activation(stat[:, 2, :], stat[:, 1, :], ACT.Sqrt, bias=eps[:, 0:1],
                           scale=1.0 / HID).then_inc(sd_ready, 1)

        @block.tensor
        def _(pe):
            pe.wait_ge(consts_made, 5)
            pe.wait_ge(x_in, 32)

            loads = [0]

            def turn_state(t, nodes):
                for c in range(CH):
                    if c >= 2:
                        pe.wait_ge(turn_out, CH * t + c - 1)
                    for m, b in enumerate(chunk(c)):
                        ins = pe.transpose(work[c % 2][0:HID, m * P:(m + 1) * P], nodes[:, b, :], ident[:])
                    ins.then_inc(turn_mm, 1)

            def terms(l):
                for c in range(CH):
                    if c >= 4:
                        pe.wait_ge(src_terms_out, CH * l + c - 3)
                        pe.wait_ge(dst_terms_out, CH * l + c - 3)
                    for m, b in enumerate(chunk(c)):
                        ins = pe.matmul(work[c % 4][:, m * P:(m + 1) * P], cat[0:HID, b * P:(b + 1) * P],
                                        w_ab[:], start=True, stop=True)
                    ins.then_inc(term_mm, 1)

            turn_state(0, xn)
            pe.wait_ge(turn_out, CH)

            pe.wait_ge(counted, 1)
            pe.matmul(work[0][0:EP, 0:NB], before[0:EP, 0:EP], count[:], start=True, stop=True)
            pe.matmul(work[1][:, 0:NB], ones[0:EP, :], count[:], start=True, stop=True).then_inc(count_mm, 1)
            pe.wait_ge(dve_step, RANKED)
            pe.wait_ge(weights_in, 16 * (GT + 9))
            terms(0)
            pe.wait_ge(src_terms_out, CH)
            pe.wait_ge(dst_terms_out, CH)
            for q in (ea_turned, term_e_mm, onehot_turned, src_gathered, terms_gathered, summed):
                pe.sem_inc(q, 2)
            with pe.Fori(0, EG // 2) as i:
                for s in range(2):
                    g = 2 * i + s
                    pe.wait_ge(ea_in[s], 16 * (i + 1))
                    pe.wait_ge(ea_t_out, reusable(g))
                    pe.transpose(work[s][:, 0:EP], ea[s][:], ident[0:EP, 0:EP]).then_inc(ea_turned, 1)
                    pe.wait_ge(ea_t_out, done(g))
                    pe.wait_ge(rec_made, 3 * g + 1)
                    pe.matmul(work[2 + s][0:EP, :], ea_t[s][:], we8[:].rearrange("p i f -> p (i f)"),
                              start=True, stop=True).then_inc(term_e_mm, 1)

            pe.wait_ge(offsets_in, 16)
            pe.wait_ge(consts_cast, 1)
            pe.wait_ge(rec_made, 3 * EG + 6)
            for l in range(2 * LAYERS):
                if 0 < l < LAYERS:
                    pe.wait_ge(state_ready, CH * l)
                    terms(l)
                if l < LAYERS:
                    pe.wait_ge(src_terms_out, CH * (l + 1))
                    pe.wait_ge(dst_terms_out, CH * (l + 1))
                if l >= LAYERS:
                    k = l - LAYERS
                    if k == 0:
                        pe.wait_ge(rel_in, 16 * 3 * LAYERS)
                        pe.wait_ge(state_ready, CH * LAYERS)
                        for c in range(ROOTS):
                            if c >= 2:
                                pe.wait_ge(back_out, c - 1)
                            for m, b in enumerate(range(8 * c, min(8 * c + 8, NB))):
                                ins = pe.transpose(work[c % 2][:, m * HID:(m + 1) * HID],
                                                   cat[0:HID, b * P:(b + 1) * P], ident[0:HID, 0:HID])
                            ins.then_inc(back_mm, 1)
                        pe.wait_ge(normed, 1)
                    else:
                        pe.wait_ge(layer_out, k)
                        pe.wait_ge(pair_in, 16 * 2 * (LAYERS - 1))
                    turn_state(1 + k, x1 if k == 0 else hn)
                    pe.wait_ge(turn_out, CH * (2 + k))
                    for b in range(NB):
                        if b >= 4:
                            pe.wait_ge(y_out, NB * k + b - 3)
                        pe.matmul(work[b % 4][:, 0:R * HID], cat[0:HID, b * P:(b + 1) * P],
                                  w_rel[k][:, 0:R, :].rearrange("i r o -> i (r o)"),
                                  start=True, stop=True).then_inc(rel_mm, 1)
                    pe.wait_ge(y_out, NB * (k + 1))
                    for c in range(ROOTS):
                        for m, b in enumerate(range(8 * c, min(8 * c + 8, NB))):
                            ins = pe.matmul(work[c][:, m * HID:(m + 1) * HID], cat[0:HID, b * P:(b + 1) * P],
                                            w_rel[k][:, R, :], start=True, stop=True)
                        ins.then_inc(root_mm, 1)
                for a in range(BANKS):
                    pe.matmul(sums_v[:, a, :], zeros_b[:, 0:P], zeros_b[:], start=True, stop=True)
                if l >= LAYERS:
                    pe.wait_ge(root_out, ROOTS * (k + 1))
                pe.wait_ge(split_ready, l + 1)

                def turn_one_hots(g, u, l=l):
                    n = l * NG + g
                    s = u % 2
                    if l > LAYERS:
                        return
                    pe.wait_ge(onehot_made, done(n))
                    pe.wait_ge(onehot_t_out, done(n - 1))
                    for j in range(GT):
                        ins = pe.transpose(turned[:, j * P:(j + 1) * P], onehot_b[s][:, j, :], ident_b[:])
                    ins.then_inc(onehot_turned, 1)

                def gather_sources(g, u, l=l):
                    n = l * NG + g
                    s = u % 2
                    pe.wait_ge(src_onehot_made, done(n))
                    pe.wait_ge(src_out, done(n - 1) if l <= LAYERS else reusable(n))
                    for m in range(GT - by_dma(l, u)):
                        source_nodes = source_one_hot(l, s, m)
                        for b in range(NB):
                            ins = pe.matmul(src_ps(l, s)[:, m * 3 * HID:(m + 1) * 3 * HID], source_nodes[:, b, :],
                                            src_split[:, b, :, :].rearrange("p k f -> p (k f)"),
                                            start=(b == 0), stop=(b == NB - 1))
                    ins.then_inc(src_gathered, 1)

                def tile_offsets(g):
                    loads[0] += 1
                    regs = [pe.alloc_register(f"off{loads[0]}_{j}") for j in range(GT)]
                    pe.load(regs, offsets[0:1, bass.ds(GT * g, GT)])
                    return regs, [pe.snap(r, min_val=0, max_val=512 * (BANKS - 1) + REC * (PER_BANK - 1))
                                  for r in regs]

                def gather_terms(g, u, l=l):
                    n = l * NG + g
                    s = u % 2
                    if l <= LAYERS:
                        regs, off = tile_offsets(g)
                    pe.wait_ge(z_ready, reusable(n))
                    if l <= LAYERS:
                        pe.wait_ge(onehot_t_out, done(n))
                        a, w = (0, HID) if l < LAYERS else (HID, R)
                        for j in range(GT):
                            ins = pe.matmul(gathered_ps[s][:, j * w:(j + 1) * w], onehot_t[s][:, j, :],
                                            terms_flat[:, bass.ds(off[j] + a, w)], start=True, stop=True)
                        for r in regs:
                            pe.free_register(r)
                    if l < LAYERS:
                        ins.then_inc(terms_gathered, 1)
                    else:
                        pe.wait_ge(src_out, done(n))
                        pe.transpose(gathered_ps[s][:, HID:HID + P], src_row[s][:], ident[:]).then_inc(src_turned, 1)

                def relate(g, u, l=l):
                    n = l * NG + g
                    s = u % 2
                    pe.wait_ge(src_t_out, n - LAYERS * NG + 1)
                    if by_dma(l, u) == GP:
                        pe.matmul(gathered_ps[s][:, R * HID:2 * R * HID], src_t[s][0:HID, :],
                                  w_rel[l - LAYERS][:, 0:R, :].rearrange("i r o -> i (r o)"),
                                  start=True, stop=True).then_inc(terms_gathered, 1)
                    else:
                        pe.matmul(gathered_ps[s][:], src_t[s][:],
                                  w_pair[:, l - LAYERS - 1, :, :].rearrange("i m w -> i (m w)"),
                                  start=True, stop=True).then_inc(terms_gathered, 1)

                def add_up(g, u, l=l):
                    n = l * NG + g
                    s = u % 2
                    regs, off = tile_offsets(g)
                    pe.wait_ge(onehot_out, done(n))
                    pe.wait_ge(msg_ready, done(n))
                    w = REC if l < LAYERS else HID
                    for j in range(GT):
                        ins = pe.matmul(sums[:, bass.ds(off[j], w)], onehot[s][:, j, :], msg[s][:, j, 0:w],
                                        start=False, stop=True, skip_group_check=True)
                    ins.then_inc(summed, 1)
                    for r in regs:
                        pe.free_register(r)

                def stage(g, u, l=l):
                    peeled = isinstance(g, int)
                    if l > LAYERS:
                        gather_terms(g, u)
                        if not peeled or g < NG - 1:
                            gather_sources(g + 1, (u + 1) % 4)
                        relate(g, u)
                        if not peeled or g > 0:
                            add_up(g - 1, (u - 1) % 4)
                        return
                    gather_sources(g, u)
                    if l < LAYERS:
                        gather_terms(g, u)
                        if not peeled or g < NG - 1:
                            turn_one_hots(g + 1, (u + 1) % 4)
                        if not peeled or g > 0:
                            add_up(g - 1, (u - 1) % 4)
                    else:
                        if not peeled or g > 0:
                            add_up(g - 1, (u - 1) % 4)
                        gather_terms(g, u)
                        if not peeled or g < NG - 1:
                            turn_one_hots(g + 1, (u + 1) % 4)
                        relate(g, u)

                turn_one_hots(0, 0)
                if l > LAYERS:
                    gather_sources(0, 0)
                stage(0, 0)
                with pe.Fori(0, QUADS - 1) as i:
                    for u in range(1, 5):
                        stage(4 * i + u, u % 4)
                for g in range(NG - 4, NG):
                    stage(g, g % 4)
                add_up(NG - 1, (NG - 1) % 4)

                if l < LAYERS:
                    pe.wait_ge(mean_ready, l + 1)
                    for c in range(CH):
                        if c >= 2:
                            pe.wait_ge(mean_t_out, CH * l + c - 1)
                        for m, b in enumerate(chunk(c)):
                            ins = pe.transpose(work[c % 2][0:HID + 1, m * P:(m + 1) * P], mean_n[:, b, :], ident[:])
                        ins.then_inc(mean_turned, 1)
                    for c in range(CH):
                        w = P * len(chunk(c))
                        pe.wait_ge(mean_t_out, CH * l + c + 1)
                        if c >= 2:
                            pe.wait_ge(agg_out, CH * l + c - 1)
                        pe.matmul(work[2 + c % 2][:, 0:w], w2e[:], mean_t[:, 512 * c:512 * c + w],
                                  start=True, stop=True).then_inc(agg_mm, 1)
                    for c in range(CH):
                        w = P * len(chunk(c))
                        pe.wait_ge(agg_out, CH * l + c + 1)
                        if c >= 2:
                            pe.wait_ge(hidden_out, CH * l + c - 1)
                        pe.matmul(work[c % 2][0:HID, 0:w], w1n[:], cat[:, 512 * c:512 * c + w],
                                  start=True, stop=True).then_inc(hidden_mm, 1)
                    for c in range(CH):
                        w = P * len(chunk(c))
                        pe.wait_ge(hidden_out, CH * l + c + 1)
                        if c >= 2:
                            pe.wait_ge(state_ready, CH * l + c - 1)
                        pe.matmul(work[2 + c % 2][0:HID, 0:w], w2n[:], hidden[:, 512 * c:512 * c + w],
                                  start=True, stop=True).then_inc(delta_mm, 1)

        @block.vector
        def _(dve):
            steps = [0]

            def step(ins):
                steps[0] += 1
                ins.then_inc(dve_step, 1)
                dve.wait_ge(dve_step, steps[0])

            for t in (xn[:, NB - 1, :], we8[:], w2e[:], no_edge[:], src_row[0][:], src_row[1][:]):
                dve.memset(t, 0.0)
            dve.memset(eps[:], EPS)
            dve.memset(zeros_b[:], 0.0)
            dve.memset(ones_e[:], 1.0)
            step(dve.memset(block_step[:], float(REC)))
            for b in range(PER_BANK - 1, NB - 1, PER_BANK):
                dve.memset(block_step[:, b:b + 1], float(512 - REC * (PER_BANK - 1)))
            dve.memset(no_edge[:, :, PLACE:TYPE + 1], -1.0).then_inc(zeroed, 1)
            dve.wait_ge(consts_made, 5)
            dve.tensor_copy(iota_b[:], iota_i[:])
            dve.tensor_copy(iota_r[:], iota_i[:, 0:R])
            dve.tensor_copy(tile_f[:], tile_i[:])
            dve.tensor_copy(node_grid[:], node_i[:].unsqueeze(2).to_broadcast([P, NB, P]))
            dve.tensor_copy(ident_b[:], ident[:]).then_inc(consts_cast, 1)
            dve.wait_ge(consts_cast, 1)

            def destination_terms(l):
                for c in range(CH):
                    dve.wait_ge(src_terms_out, CH * l + c + 1)
                    for m, b in enumerate(chunk(c)):
                        at = REC * (b % PER_BANK)
                        ins = dve.tensor_copy(dst_terms[:, b // PER_BANK, at:at + HID],
                                              work[c % 4][:, m * P + HID:(m + 1) * P])
                    ins.then_inc(dst_terms_out, 1)

            dve.wait_ge(edges_in, 48)
            step(dve.tensor_scalar(part_i, dst_i, 7, None, ALU.logical_shift_right))
            step(dve.tensor_copy(block_f, part_i))
            step(dve.tensor_scalar(part_i, dst_i, P - 1, None, ALU.bitwise_and))
            dve.tensor_copy(meta[:, :, PLACE - HID], part_i)
            dve.tensor_copy(meta[:, :, TYPE - HID], type_i)
            dve.tensor_copy(meta_i[:, :, ROW0 - HID], src_i)
            dve.scalar_tensor_tensor(out=meta_i[:, :, ROW1 - HID], in0=src_i, scalar=float(R), in1=type_i,
                                     op0=ALU.mult, op1=ALU.add)
            for k in range(NB):
                ins = dve.tensor_scalar(in_block[:, k, :], block_f, float(k), None, ALU.is_equal, ALU.add,
                                        accum_out=count[:, k:k + 1])
            ins.then_inc(counted, 1)
            dve.wait_ge(count_mm, 1)
            step(dve.tensor_scalar(tiles_i[:], work[1][:, 0:NB], float(P - 1), None, ALU.add))
            step(dve.tensor_scalar(tiles_i[:], tiles_i[:], 7, None, ALU.logical_shift_right))
            step(dve.tensor_copy(tiles_f[:], tiles_i[:]))
            step(dve.tensor_tensor_scan(tiles_end[:], ones[:, 0:NB], tiles_f[:], 0.0, ALU.mult, ALU.add))
            step(dve.tensor_tensor(first_slot[:], tiles_end[:], tiles_f[:], ALU.subtract))
            step(dve.tensor_scalar(first_slot[:], first_slot[:], float(P), -1.0, ALU.mult, ALU.add))
            step(dve.tensor_tensor(first_slot[0:EP, :], first_slot[0:EP, :], work[0][0:EP, 0:NB], ALU.add))
            assert steps[0] == RANKED
            step(dve.tensor_tensor(passed[:], tile_f[:].unsqueeze(2).to_broadcast([P, GT, NB - 1]),
                                   tiles_end[:, 0:NB - 1].unsqueeze(1).to_broadcast([P, GT, NB - 1]), ALU.is_ge))
            step(dve.tensor_tensor(passed[:], passed[:],
                                   block_step[:].unsqueeze(1).to_broadcast([P, GT, NB - 1]), ALU.mult))
            step(dve.tensor_reduce(off_f[:], passed[:], X_AXIS, ALU.add))
            dve.tensor_copy(off_i[:], off_f[:]).then_inc(off_ready, 1)
            def rank_block(k, a, b):
                step(dve.tensor_tensor_scan(rank[:, a:b], ones_e[0:EP, a:b], in_block[:, k, a:b],
                                            first_slot[0:EP, k:k + 1], ALU.mult, ALU.add))
                ins = dve.copy_predicated(slot_f[:, a:b], in_block[:, k, a:b].bitcast(U16), rank[:, a:b])
                if b < EC:
                    ins = dve.tensor_copy(first_slot[0:EP, k:k + 1], rank[:, b - 1:b])
                step(ins)

            def slot_rows(a, b):
                at, slot, part = addr[:, a:b], slot_i[:, a:b], part_i[:, a:b]
                step(dve.tensor_copy(slot, slot_f[:, a:b]))
                step(dve.tensor_scalar(at, slot, ((1 << 21) - 1) & ~(GT * P - 1), None, ALU.bitwise_and))
                step(dve.tensor_scalar(part, slot, P - 1, 3, ALU.bitwise_and, ALU.logical_shift_left))
                step(dve.tensor_tensor(at, at, part, ALU.bitwise_or))
                step(dve.tensor_scalar(part, slot, 7, GT - 1, ALU.logical_shift_right, ALU.bitwise_and))
                step(dve.tensor_tensor(at, at, part, ALU.bitwise_or))

            for k in range(NB):
                if k == NB // 2:
                    destination_terms(0)
                rank_block(k, 0, EARLY * GT)
            slot_rows(0, EARLY * GT)

            def make_records(g, i, s, first):
                dve.wait_ge(term_e_mm, done(g))
                if not first:
                    dve.wait_ge(rec_stored[s], 16 * GT * i)
                dve.tensor_tensor(rec_out[s][:, :, 0:HID],
                                  work[2 + s][0:EP, :].rearrange("p (j f) -> p j f", j=GT),
                                  b1e_all[0:EP, :].unsqueeze(1).to_broadcast([EP, GT, HID]),
                                  ALU.add).then_inc(rec_made, 1)
                dve.tensor_copy(rec_out[s][:, :, HID:REC].bitcast(I32),
                                meta_i[:, bass.ds(GT * g, GT), :]).then_inc(rec_made, 1)
                dve.tensor_copy(addr_out[s][:], addr[:, bass.ds(GT * g, GT)]).then_inc(rec_made, 1)

            dve.sem_inc(rec_made, 6)
            for i in range(EARLY // 2):
                for s in range(2):
                    make_records(2 * i + s, i, s, i == 0)
                for k in range(RANKED_PER_PAIR * i, min(RANKED_PER_PAIR * (i + 1), NB)):
                    rank_block(k, EARLY * GT, EC)
            slot_rows(EARLY * GT, EC)
            with dve.Fori(EARLY // 2, EG // 2) as i:
                for s in range(2):
                    make_records(2 * i + s, i, s, False)
            dve.wait_ge(rec_made, 3 * EG + 6)

            for q in (onehot_made, src_onehot_made, src_out, z_ready, msg_ready):
                dve.sem_inc(q, 2)
            dve.sem_inc(rec_used, RECS)

            def split(nodes):
                step(dve.tensor_copy(src_split[:, :, 0, :], nodes))
                step(dve.tensor_tensor(v, nodes, src_split[:, :, 0, :], ALU.subtract))
                step(dve.tensor_copy(src_split[:, :, 1, :], v))
                step(dve.tensor_tensor(v, v, src_split[:, :, 1, :], ALU.subtract))
                dve.tensor_copy(src_split[:, :, 2, :], v).then_inc(split_ready, 1)

            def norm(t, res):
                step(dve.tensor_reduce(stat[:, 0, :], v, X_AXIS, ALU.add))
                step(dve.tensor_scalar(stat[:, 0, :], stat[:, 0, :], 1.0 / HID, None, ALU.mult))
                step(dve.tensor_tensor(v, v, stat[:, 0, :].unsqueeze(2).to_broadcast([P, NB, HID]), ALU.subtract))
                step(dve.tensor_tensor(res[:], v, v, ALU.mult))
                dve.tensor_reduce(stat[:, 1, :], res[:], X_AXIS, ALU.add).then_inc(var_ready, 1)
                dve.wait_ge(sd_ready, t)
                step(dve.reciprocal(stat[:, 3, :], stat[:, 2, :]))
                dve.tensor_tensor(res[:], v, stat[:, 3, :].unsqueeze(2).to_broadcast([P, NB, HID]),
                                  ALU.mult).then_inc(normed, 1)

            for l in range(2 * LAYERS):
                if 0 < l < LAYERS:
                    destination_terms(l)
                if l >= LAYERS:
                    k = l - LAYERS
                    if k == 0:
                        for c in range(ROOTS):
                            n = min(8, NB - 8 * c)
                            dve.wait_ge(back_mm, c + 1)
                            dve.tensor_tensor(v[:, 8 * c:8 * c + n, :],
                                              work[c % 2][:, 0:n * HID].rearrange("p (b f) -> p b f", b=n),
                                              xn[:, 8 * c:8 * c + n, :], ALU.add).then_inc(back_out, 1)
                        dve.wait_ge(back_out, ROOTS)
                        norm(1, x1)
                        dve.memset(w_pair, 0.0).then_inc(pair_zeroed, 1)
                        dve.wait_ge(rel_in, 16 * 3 * LAYERS)
                if l < LAYERS:
                    dve.wait_ge(src_terms_out, CH * (l + 1))
                elif l == LAYERS:
                    dve.wait_ge(normed, 1)
                else:
                    dve.wait_ge(layer_out, k)
                split(hn[:] if l != LAYERS else x1[:])
                if l == 0:
                    dve.wait_ge(src_cols_in, 32)
                    dve.tensor_copy(src_cols16, src_cols.bitcast(I32)).then_inc(src_cols_cast, 1)
                if l >= LAYERS:
                    for c in range(ROOTS):
                        n = min(8, NB - 8 * c)
                        dve.wait_ge(root_mm, ROOTS * k + c + 1)
                        dve.tensor_tensor(root[:, 8 * c:8 * c + n, :],
                                          work[c][:, 0:n * HID].rearrange("p (b f) -> p b f", b=n),
                                          b_rel[k][:].unsqueeze(1).to_broadcast([P, n, HID]),
                                          ALU.add).then_inc(root_out, 1)

                def one_hots(i, u, l=l):
                    n = l * NG + 4 * i + u
                    s = u % 2
                    rec = rec_in[u]
                    dve.wait_ge(rec_loaded[u], 16 * (l * USES[u] + i + 1))
                    if l <= LAYERS:
                        dve.wait_ge(onehot_turned, reusable(n))
                    dve.wait_ge(onehot_out, reusable(n))
                    for j in range(GT):
                        ins = dve.tensor_scalar(onehot_b[s][:, j, :], iota_b[:], rec[:, j, PLACE:PLACE + 1], None,
                                                ALU.is_equal)
                    ins.then_inc(onehot_made, 1)
                    if l <= LAYERS:
                        source_one_hots(i, u)

                def source_one_hots(i, u, l=l):
                    n = l * NG + 4 * i + u
                    s = u % 2
                    dve.wait_ge(src_loaded[u], 16 * (l * USES[u] + i + 1))
                    dve.wait_ge(src_gathered, reusable(n))
                    for m in range(GT - by_dma(l, u)):
                        ins = dve.tensor_tensor(source_one_hot(l, s, m),
                                                src_in[u][:, m:m + 1, :].to_broadcast([P, NB, P]), node_grid[:],
                                                ALU.is_equal)
                    ins.then_inc(src_onehot_made, 1)

                def source_sum(i, u, l=l):
                    m = GT - by_dma(l, u)
                    n = l * NG + 4 * i + u
                    s = u % 2
                    dve.wait_ge(src_gathered, done(n))
                    if l >= LAYERS:
                        dve.wait_ge(terms_gathered, reusable(n))
                    dve.tensor_reduce(src_row[s][:, 0:m * HID].rearrange("p (m f) -> p m f", m=m),
                                      src_ps(l, s)[:, 0:m * 3 * HID].rearrange("p (m k f) -> p m f k", m=m, k=3),
                                      X_AXIS, ALU.add).then_inc(src_out, 1)

                def messages(i, u, nt, l=l):
                    n = l * NG + 4 * i + u
                    s = u % 2
                    rec = rec_in[u]
                    types = rec[:, :, TYPE:TYPE + 1].to_broadcast([P, GT, R])
                    type_row = iota_r[:].unsqueeze(1).to_broadcast([P, GT, R])
                    dve.wait_ge(summed, reusable(n))
                    if l < LAYERS:
                        dve.tensor_tensor(msg[s][:, :, HID:REC], type_row, types, ALU.is_equal)
                        source_sum(i, u)
                        dve.wait_ge(rows_in[s], rows_landed(l, i, u, nt))
                        dve.wait_ge(msg_ready, reusable(n))
                        nd = by_dma(l, u)
                        dve.tensor_tensor(z[s][:, 0:nd, :], rows[s][:, 0:nd, :], rec[:, 0:nd, 0:HID], ALU.add)
                        dve.wait_ge(src_out, done(n))
                        for m in range(GT - nd):
                            ins = dve.tensor_tensor(z[s][:, GT - 1 - m, :], src_row[s][:, m * HID:(m + 1) * HID],
                                                    rec[:, GT - 1 - m, 0:HID], ALU.add)
                        ins.then_inc(rec_used, 1)
                        dve.wait_ge(terms_gathered, done(n))
                        dve.wait_ge(rec_used, done(n, RECS))
                        dve.tensor_tensor(z[s][:], z[s][:], gathered_ps[s][:].rearrange("p (j f) -> p j f", j=GT),
                                          ALU.add).then_inc(z_ready, 1)
                    else:
                        k = l - LAYERS
                        m = 4 * (n - LAYERS * NG)
                        slots = weight[:, bass.ds(GT * (n - l * NG), GT), :]
                        nd = by_dma(l, u)
                        last = weight[:, bass.ds(GT * (n - l * NG) + nd, GT - nd), :].rearrange("p a r -> p (a r)")
                        if k == 0:
                            dve.tensor_tensor(is_type[s][:], type_row, types, ALU.is_equal).then_inc(share_step, 1)
                            dve.wait_ge(share_step, m + 1)
                            dve.wait_ge(terms_gathered, done(n))
                            dve.tensor_tensor(slots, is_type[s][:],
                                              gathered_ps[s][:, 0:GT * R].rearrange("p (j r) -> p j r", j=GT),
                                              ALU.mult).then_inc(share_step, 1)
                        else:
                            dve.wait_ge(terms_gathered, done(n))
                            dve.sem_inc(share_step, 2)
                        dve.wait_ge(share_step, m + 2)
                        rows_by_type = by_type[s][:].rearrange("p m r f -> p (m r) f")[:, 0:(GT - nd) * R, :]
                        dve.tensor_tensor(rows_by_type,
                                          gathered_ps[s][:, (nd - GP + 1) * R * HID:2 * R * HID]
                                          .rearrange("p (r f) -> p r f", f=HID),
                                          last.unsqueeze(2).to_broadcast([P, (GT - nd) * R, HID]),
                                          ALU.mult).then_inc(z_ready, 1)
                        dve.tensor_reduce(share[s][:], slots, X_AXIS, ALU.add).then_inc(share_step, 1)
                        dve.wait_ge(z_ready, done(n))
                        dve.tensor_reduce(msg[s][:, nd:GT, 0:HID],
                                          rows_by_type.rearrange("p (m r) f -> p m f r", r=R),
                                          X_AXIS, ALU.add).then_inc(share_step, 1)
                        dve.wait_ge(share_step, m + 3)
                        dve.wait_ge(rows_in[s], rows_landed(l, i, u, nt))
                        dve.tensor_tensor(msg[s][:, 0:nd, 0:HID], rows[s][:, 0:nd, :],
                                          share[s][:, 0:nd].unsqueeze(2).to_broadcast([P, nd, HID]),
                                          ALU.mult).then_inc(msg_ready, 1)
                        dve.wait_ge(msg_ready, done(n))
                        dve.sem_inc(rec_used, 1)

                def group(i, u, nt):
                    if nt == GP:
                        one_hots(i + (u + 1) // 4, (u + 1) % 4)
                        if not (isinstance(i, int) and i == QUADS - 1 and u == 3):
                            source_one_hots(i + (u + 2) // 4, (u + 2) % 4)
                        source_sum(i + (u + 1) // 4, (u + 1) % 4)
                    messages(i, u, nt)

                if l <= LAYERS:
                    staged_groups(dve, one_hots, messages, before=source_sum if l == LAYERS else None)
                else:
                    source_one_hots(0, 0)
                    one_hots(0, 0)
                    source_one_hots(0, 1)
                    source_sum(0, 0)
                    with dve.Fori(0, QUADS - 1) as i:
                        for u in range(4):
                            group(i, u, GP)
                    for u in range(4):
                        group(QUADS - 1, u, GP)
                    group(QUADS, 0, LAST_TILES)
                dve.wait_ge(summed, done(l * NG + NG - 1))

                if l < LAYERS:
                    for c in range(BANKS):
                        bs = bank_blocks(c)
                        ins = dve.tensor_reduce(deg[:, 0, bs[0]:bs[-1] + 1], bank_view(sums_v, c, HID, REC),
                                                X_AXIS, ALU.add)
                    step(ins)
                    dve.tensor_scalar(mean_n[:, :, HID], deg[:, 0, :], 1.0, None, ALU.min)
                    step(dve.tensor_scalar(deg[:, 1, :], deg[:, 0, :], 1.0, None, ALU.max))
                    step(dve.reciprocal(deg[:, 2, :], deg[:, 1, :]))
                    for c in range(BANKS):
                        bs = bank_blocks(c)
                        ins = dve.tensor_tensor(mean_n[:, bs[0]:bs[-1] + 1, 0:HID], bank_view(sums_v, c, 0, HID),
                                                deg[:, 2, bs[0]:bs[-1] + 1].unsqueeze(2)
                                                .to_broadcast([P, len(bs), HID]), ALU.mult)
                        if l == LAYERS - 1:
                            ins = dve.tensor_scalar(bank_view(dst_terms, c, HID, REC), bank_view(sums_v, c, HID, REC),
                                                    1.0, None, ALU.max)
                    if l == LAYERS - 1:
                        step(ins)
                        for c in range(BANKS):
                            ins = dve.reciprocal(bank_view(dst_terms, c, HID, REC), bank_view(dst_terms, c, HID, REC))
                    ins.then_inc(mean_ready, 1)
                    for c in range(CH):
                        w = P * len(chunk(c))
                        dve.wait_ge(delta_mm, CH * l + c + 1)
                        at = cat[0:HID, 512 * c:512 * c + w]
                        dve.scalar_tensor_tensor(out=at, in0=work[2 + c % 2][0:HID, 0:w], scalar=b2n_c[:, 0:1],
                                                 in1=at, op0=ALU.add, op1=ALU.add).then_inc(state_ready, 1)
                else:
                    to = v if k == LAYERS - 1 else hn[:]
                    for c in range(BANKS):
                        bs = bank_blocks(c)
                        ins = dve.tensor_tensor(to[:, bs[0]:bs[-1] + 1, :], bank_view(sums_v, c, 0, HID),
                                                root[:, bs[0]:bs[-1] + 1, :], ALU.add)
                    step(ins)
                    if k < LAYERS - 1:
                        dve.tensor_scalar(hn[:], hn[:], 0.0, None, ALU.max).then_inc(layer_out, 1)
                    else:
                        step(dve.tensor_tensor(v, v, x1[:], ALU.add))
                        norm(2, hn)


RANKED = 11


_L0 = ['L0_gnn_' + n for n in ('W1e', 'b1e', 'W2e', 'b2e', 'W1n', 'b1n', 'W2n', 'b2n')]
_INS = ['x', 'src', 'dst', 'edge_attr_16', 'edge_type_4'] + _L0 + [
    f'L1_gnn_{n}{l}' for n in ('W', 'root', 'b') for l in range(3)]


def kernel(**inputs):
    import numpy as _np
    import concourse.bacc as _bacc
    from concourse import mybir as _mybir
    from concourse.bass_utils import run_bass_kernel_spmd as _run

    nc = _bacc.Bacc("TRN2", target_bir_lowering=False, num_devices=1)
    arrays, args = {}, []
    for name in _INS:
        a = _np.ascontiguousarray(inputs[name])
        arrays[f"in_{name}_dram"] = a
        args.append(nc.dram_tensor(f"in_{name}_dram", a.shape, _mybir.dt.from_np(a.dtype), kind="ExternalInput").ap())
    out = nc.dram_tensor("out_0_dram", args[0].shape, _mybir.dt.float32, kind="ExternalOutput").ap()
    gnn_kernel(nc, *args[:13], args[13:16], args[16:19], args[19:22], out)
    r = _run(nc, [arrays], core_ids=[0])
    return r.results[0]["out_0_dram"]
```
